# Optimizing a Trainium2 kernel written in Bass

```python
import numpy as np
import jax
import jax.numpy as jnp

def _softmax(x, axis=-1):
    return jax.nn.softmax(x, axis=axis)

def _gelu(x):
    return jax.nn.gelu(x, approximate=True)

def _silu(x):
    return jax.nn.silu(x)

def _sigmoid(x):
    return jax.nn.sigmoid(x)

def _layernorm(x, axis=-1, eps=1e-05):
    m = jnp.mean(x, axis=axis, keepdims=True)
    v = jnp.var(x, axis=axis, keepdims=True)
    return (x - m) / jnp.sqrt(v + eps)

def _scatter_add(tgt, idx, src, axis=0):
    return tgt.at[idx].add(src)

def _segment_sum(src, seg, n):
    return jax.ops.segment_sum(src, seg, n)
kernel_name = 'mk_dlrm_tower_d1_rec_r8_499f8b'

def setup_inputs(seed: int=0):
    np.random.seed(seed)
    _w = jnp.asarray

    def _rec_inputs():
        import jax
        import jax.numpy as jnp
        _tk = jax.random.key(seed)
        dense_ctx = jax.random.normal(jax.random.fold_in(_tk, 190), (1024, 16), jnp.float32)
        ids = jnp.stack([jax.random.randint(jax.random.fold_in(_tk, 200 + f), (1024,), 0, v, jnp.int32) for f, v in enumerate([12500, 125000, 12500, 125000, 125000, 1000, 1250, 12500, 125000, 12500, 125000, 1250, 1250, 1250, 1000, 125000, 1000, 125000, 12500, 125000, 12500, 125000, 12500, 1000, 125000, 125000, 125000, 125000, 125000, 12500, 1250, 12500, 12500, 12500, 1250, 12500, 1250, 12500, 1250])], axis=1)
        tbl_0 = 0.05 * jax.random.normal(jax.random.fold_in(_tk, 500 + 0), (12500, 16), jnp.float32)
        tbl_1 = 0.05 * jax.random.normal(jax.random.fold_in(_tk, 500 + 1), (125000, 16), jnp.float32)
        tbl_2 = 0.05 * jax.random.normal(jax.random.fold_in(_tk, 500 + 2), (12500, 16), jnp.float32)
        tbl_3 = 0.05 * jax.random.normal(jax.random.fold_in(_tk, 500 + 3), (125000, 16), jnp.float32)
        tbl_4 = 0.05 * jax.random.normal(jax.random.fold_in(_tk, 500 + 4), (125000, 16), jnp.float32)
        tbl_5 = 0.05 * jax.random.normal(jax.random.fold_in(_tk, 500 + 5), (1000, 16), jnp.float32)
        tbl_6 = 0.05 * jax.random.normal(jax.random.fold_in(_tk, 500 + 6), (1250, 16), jnp.float32)
        tbl_7 = 0.05 * jax.random.normal(jax.random.fold_in(_tk, 500 + 7), (12500, 16), jnp.float32)
        tbl_8 = 0.05 * jax.random.normal(jax.random.fold_in(_tk, 500 + 8), (125000, 16), jnp.float32)
        tbl_9 = 0.05 * jax.random.normal(jax.random.fold_in(_tk, 500 + 9), (12500, 16), jnp.float32)
        tbl_10 = 0.05 * jax.random.normal(jax.random.fold_in(_tk, 500 + 10), (125000, 16), jnp.float32)
        tbl_11 = 0.05 * jax.random.normal(jax.random.fold_in(_tk, 500 + 11), (1250, 16), jnp.float32)
        tbl_12 = 0.05 * jax.random.normal(jax.random.fold_in(_tk, 500 + 12), (1250, 16), jnp.float32)
        tbl_13 = 0.05 * jax.random.normal(jax.random.fold_in(_tk, 500 + 13), (1250, 16), jnp.float32)
        tbl_14 = 0.05 * jax.random.normal(jax.random.fold_in(_tk, 500 + 14), (1000, 16), jnp.float32)
        tbl_15 = 0.05 * jax.random.normal(jax.random.fold_in(_tk, 500 + 15), (125000, 16), jnp.float32)
        tbl_16 = 0.05 * jax.random.normal(jax.random.fold_in(_tk, 500 + 16), (1000, 16), jnp.float32)
        tbl_17 = 0.05 * jax.random.normal(jax.random.fold_in(_tk, 500 + 17), (125000, 16), jnp.float32)
        tbl_18 = 0.05 * jax.random.normal(jax.random.fold_in(_tk, 500 + 18), (12500, 16), jnp.float32)
        tbl_19 = 0.05 * jax.random.normal(jax.random.fold_in(_tk, 500 + 19), (125000, 16), jnp.float32)
        tbl_20 = 0.05 * jax.random.normal(jax.random.fold_in(_tk, 500 + 20), (12500, 16), jnp.float32)
        tbl_21 = 0.05 * jax.random.normal(jax.random.fold_in(_tk, 500 + 21), (125000, 16), jnp.float32)
        tbl_22 = 0.05 * jax.random.normal(jax.random.fold_in(_tk, 500 + 22), (12500, 16), jnp.float32)
        tbl_23 = 0.05 * jax.random.normal(jax.random.fold_in(_tk, 500 + 23), (1000, 16), jnp.float32)
        tbl_24 = 0.05 * jax.random.normal(jax.random.fold_in(_tk, 500 + 24), (125000, 16), jnp.float32)
        tbl_25 = 0.05 * jax.random.normal(jax.random.fold_in(_tk, 500 + 25), (125000, 16), jnp.float32)
        tbl_26 = 0.05 * jax.random.normal(jax.random.fold_in(_tk, 500 + 26), (125000, 16), jnp.float32)
        tbl_27 = 0.05 * jax.random.normal(jax.random.fold_in(_tk, 500 + 27), (125000, 16), jnp.float32)
        tbl_28 = 0.05 * jax.random.normal(jax.random.fold_in(_tk, 500 + 28), (125000, 16), jnp.float32)
        tbl_29 = 0.05 * jax.random.normal(jax.random.fold_in(_tk, 500 + 29), (12500, 16), jnp.float32)
        tbl_30 = 0.05 * jax.random.normal(jax.random.fold_in(_tk, 500 + 30), (1250, 16), jnp.float32)
        tbl_31 = 0.05 * jax.random.normal(jax.random.fold_in(_tk, 500 + 31), (12500, 16), jnp.float32)
        tbl_32 = 0.05 * jax.random.normal(jax.random.fold_in(_tk, 500 + 32), (12500, 16), jnp.float32)
        tbl_33 = 0.05 * jax.random.normal(jax.random.fold_in(_tk, 500 + 33), (12500, 16), jnp.float32)
        tbl_34 = 0.05 * jax.random.normal(jax.random.fold_in(_tk, 500 + 34), (1250, 16), jnp.float32)
        tbl_35 = 0.05 * jax.random.normal(jax.random.fold_in(_tk, 500 + 35), (12500, 16), jnp.float32)
        tbl_36 = 0.05 * jax.random.normal(jax.random.fold_in(_tk, 500 + 36), (1250, 16), jnp.float32)
        tbl_37 = 0.05 * jax.random.normal(jax.random.fold_in(_tk, 500 + 37), (12500, 16), jnp.float32)
        tbl_38 = 0.05 * jax.random.normal(jax.random.fold_in(_tk, 500 + 38), (1250, 16), jnp.float32)
        _rk = jax.random.fold_in(_tk, 7)
        W_top1 = 0.05 * jax.random.normal(jax.random.fold_in(_tk, 801), (400, 512), jnp.float32)
        W_top2 = 0.0441942 * jax.random.normal(jax.random.fold_in(_tk, 802), (512, 256), jnp.float32)
        W_top3 = 0.0625 * jax.random.normal(jax.random.fold_in(_tk, 803), (256, 1), jnp.float32)
        b_top1 = jnp.zeros((512,), jnp.float32)
        b_top2 = jnp.zeros((256,), jnp.float32)
        return (dense_ctx, ids, tbl_0, tbl_1, tbl_2, tbl_3, tbl_4, tbl_5, tbl_6, tbl_7, tbl_8, tbl_9, tbl_10, tbl_11, tbl_12, tbl_13, tbl_14, tbl_15, tbl_16, tbl_17, tbl_18, tbl_19, tbl_20, tbl_21, tbl_22, tbl_23, tbl_24, tbl_25, tbl_26, tbl_27, tbl_28, tbl_29, tbl_30, tbl_31, tbl_32, tbl_33, tbl_34, tbl_35, tbl_36, tbl_37, tbl_38, W_top1, b_top1, W_top2, b_top2, W_top3)
    dense_ctx, ids, tbl_0, tbl_1, tbl_2, tbl_3, tbl_4, tbl_5, tbl_6, tbl_7, tbl_8, tbl_9, tbl_10, tbl_11, tbl_12, tbl_13, tbl_14, tbl_15, tbl_16, tbl_17, tbl_18, tbl_19, tbl_20, tbl_21, tbl_22, tbl_23, tbl_24, tbl_25, tbl_26, tbl_27, tbl_28, tbl_29, tbl_30, tbl_31, tbl_32, tbl_33, tbl_34, tbl_35, tbl_36, tbl_37, tbl_38, W_top1, b_top1, W_top2, b_top2, W_top3 = _rec_inputs()

    def _L0_rec_setup():
        import jax, jax.numpy as jnp
        import numpy as np
        B, F0, D = (256, 39, 16)
        CROSS = [128, 128, 128]
        key = jax.random.key(seed)
        k0, k1, k2, k3 = jax.random.split(key, 4)
        inputs = jax.random.normal(k0, (B, F0, D), dtype=jnp.float32)
        f0 = jax.random.normal(k1, (F0 * F0, CROSS[0]), dtype=jnp.float32) * 0.05
        f1 = jax.random.normal(k2, (CROSS[0] * F0, CROSS[1]), dtype=jnp.float32) * 0.05
        f2 = jax.random.normal(k3, (CROSS[1] * F0, CROSS[2]), dtype=jnp.float32) * 0.05
        return {'inputs': inputs, 'f0': f0, 'f1': f1, 'f2': f2}
    _L0_rec_all = _L0_rec_setup()
    _L0_rec_in = {k: v for k, v in _L0_rec_all.items() if k in ('f0', 'f1', 'f2')}
    del _L0_rec_all
    return {'dense_ctx': dense_ctx, 'ids': ids, 'tbl_0': tbl_0, 'tbl_1': tbl_1, 'tbl_2': tbl_2, 'tbl_3': tbl_3, 'tbl_4': tbl_4, 'tbl_5': tbl_5, 'tbl_6': tbl_6, 'tbl_7': tbl_7, 'tbl_8': tbl_8, 'tbl_9': tbl_9, 'tbl_10': tbl_10, 'tbl_11': tbl_11, 'tbl_12': tbl_12, 'tbl_13': tbl_13, 'tbl_14': tbl_14, 'tbl_15': tbl_15, 'tbl_16': tbl_16, 'tbl_17': tbl_17, 'tbl_18': tbl_18, 'tbl_19': tbl_19, 'tbl_20': tbl_20, 'tbl_21': tbl_21, 'tbl_22': tbl_22, 'tbl_23': tbl_23, 'tbl_24': tbl_24, 'tbl_25': tbl_25, 'tbl_26': tbl_26, 'tbl_27': tbl_27, 'tbl_28': tbl_28, 'tbl_29': tbl_29, 'tbl_30': tbl_30, 'tbl_31': tbl_31, 'tbl_32': tbl_32, 'tbl_33': tbl_33, 'tbl_34': tbl_34, 'tbl_35': tbl_35, 'tbl_36': tbl_36, 'tbl_37': tbl_37, 'tbl_38': tbl_38, 'W_top1': W_top1, 'b_top1': b_top1, 'W_top2': W_top2, 'b_top2': b_top2, 'W_top3': W_top3, 'L0_rec_f0': _L0_rec_in['f0'], 'L0_rec_f1': _L0_rec_in['f1'], 'L0_rec_f2': _L0_rec_in['f2']}

def reference(dense_ctx, ids, tbl_0, tbl_1, tbl_2, tbl_3, tbl_4, tbl_5, tbl_6, tbl_7, tbl_8, tbl_9, tbl_10, tbl_11, tbl_12, tbl_13, tbl_14, tbl_15, tbl_16, tbl_17, tbl_18, tbl_19, tbl_20, tbl_21, tbl_22, tbl_23, tbl_24, tbl_25, tbl_26, tbl_27, tbl_28, tbl_29, tbl_30, tbl_31, tbl_32, tbl_33, tbl_34, tbl_35, tbl_36, tbl_37, tbl_38, W_top1, b_top1, W_top2, b_top2, W_top3, L0_rec_f0, L0_rec_f1, L0_rec_f2):
    import jax
    import jax.numpy as jnp

    def _L0_rec_ref(inputs, f0, f1, f2):
        import jax, jax.numpy as jnp
        import numpy as np
        B, F0, D = (256, 39, 16)
        CROSS = [128, 128, 128]
        filters = [f0, f1, f2]
        x0 = inputs
        xk = inputs
        outs = []
        for W in filters:
            b, f, d = x0.shape
            g = xk.shape[1]
            z = jnp.einsum('bfd,bgd->bfgd', x0, xk).reshape(b, f * g, d)
            cur = jnp.einsum('bpd,pm->bmd', z, W)
            outs.append(cur)
            xk = cur
        result = jnp.concatenate(outs, axis=1)
        return jnp.sum(result, axis=-1)
    e = jnp.stack([tbl_0[ids[:, 0]], tbl_1[ids[:, 1]], tbl_2[ids[:, 2]], tbl_3[ids[:, 3]], tbl_4[ids[:, 4]], tbl_5[ids[:, 5]], tbl_6[ids[:, 6]], tbl_7[ids[:, 7]], tbl_8[ids[:, 8]], tbl_9[ids[:, 9]], tbl_10[ids[:, 10]], tbl_11[ids[:, 11]], tbl_12[ids[:, 12]], tbl_13[ids[:, 13]], tbl_14[ids[:, 14]], tbl_15[ids[:, 15]], tbl_16[ids[:, 16]], tbl_17[ids[:, 17]], tbl_18[ids[:, 18]], tbl_19[ids[:, 19]], tbl_20[ids[:, 20]], tbl_21[ids[:, 21]], tbl_22[ids[:, 22]], tbl_23[ids[:, 23]], tbl_24[ids[:, 24]], tbl_25[ids[:, 25]], tbl_26[ids[:, 26]], tbl_27[ids[:, 27]], tbl_28[ids[:, 28]], tbl_29[ids[:, 29]], tbl_30[ids[:, 30]], tbl_31[ids[:, 31]], tbl_32[ids[:, 32]], tbl_33[ids[:, 33]], tbl_34[ids[:, 34]], tbl_35[ids[:, 35]], tbl_36[ids[:, 36]], tbl_37[ids[:, 37]], tbl_38[ids[:, 38]]], axis=1)
    z = _L0_rec_ref(e, L0_rec_f0, L0_rec_f1, L0_rec_f2)
    z = z.reshape(z.shape[0], -1)
    h = jnp.concatenate([z, dense_ctx], axis=1)
    h = jnp.maximum(h @ W_top1 + b_top1, 0.0)
    h = jnp.maximum(h @ W_top2 + b_top2, 0.0)
    y = h @ W_top3
    return y

_drawn_inputs = setup_inputs


def setup_inputs(seed=0):
    import zlib

    import numpy as np

    out = dict(_drawn_inputs(seed))
    spreads = {'b_top1': (0.0, 0.565), 'b_top2': (0.0, 0.1)}
    factors = {'tbl_0': 4.648,
     'tbl_1': 4.816,
     'tbl_2': 4.633,
     'tbl_3': 4.858,
     'tbl_4': 4.898,
     'tbl_5': 4.799,
     'tbl_6': 4.536,
     'tbl_7': 4.687,
     'tbl_8': 4.926,
     'tbl_9': 4.233,
     'tbl_10': 5.019,
     'tbl_11': 4.608,
     'tbl_12': 4.156,
     'tbl_13': 4.348,
     'tbl_14': 4.587,
     'tbl_15': 4.771,
     'tbl_16': 5.014,
     'tbl_17': 4.492,
     'tbl_18': 4.836,
     'tbl_19': 4.947,
     'tbl_20': 4.85,
     'tbl_21': 4.795,
     'tbl_22': 4.634,
     'tbl_23': 4.84,
     'tbl_24': 4.435,
     'tbl_25': 4.522,
     'tbl_26': 4.593,
     'tbl_27': 4.927,
     'tbl_28': 4.683,
     'tbl_29': 4.836,
     'tbl_30': 4.79,
     'tbl_31': 4.316,
     'tbl_32': 4.835,
     'tbl_33': 4.894,
     'tbl_34': 4.487,
     'tbl_35': 4.6,
     'tbl_36': 4.818,
     'tbl_37': 4.818,
     'tbl_38': 5.063,
     'L0_rec_f1': 5.039,
     'L0_rec_f2': 8.0}
    for name, (base, spread) in spreads.items():
        noise = np.random.default_rng([zlib.crc32(name.encode()), seed]).standard_normal(out[name].shape)
        drawn = base * np.exp(spread * noise) if base else spread * noise
        out[name] = jnp.asarray(drawn.astype(out[name].dtype))
    for name, factor in factors.items():
        out[name] = (out[name] * factor).astype(out[name].dtype)
    return out
```

```python
import concourse.bass as bass
from concourse import mybir
from contextlib import ExitStack


class Linear:

    def __init__(self, register, times, plus):
        self.register, self.times, self.plus = register, times, plus

    def __add__(self, k):
        return Linear(self.register, self.times, self.plus + k)

    def __sub__(self, k):
        return self + -k

    def __mul__(self, k):
        return Linear(self.register, self.times * k, self.plus * k)

    __radd__, __rmul__ = __add__, __mul__


def value(x):
    return x if isinstance(x, int) else x.register * x.times + x.plus


def build_cin_tower(nc, dense_ctx, ids, tables, W_top1, b_top1, W_top2, b_top2, W_top3, f0, f1, f2, out):
    fp32 = mybir.dt.float32
    ALU = mybir.AluOpType
    ACT = mybir.ActivationFunctionType
    AX = mybir.AxisListType
    AP = bass.AP

    B, F = ids.shape
    D = tables[0].shape[1]
    M = f0.shape[1]
    P = 128
    CHUNKS = B // P
    GRP = 4
    DB = D // GRP
    N = P // GRP * D
    GROUPS = CHUNKS * GRP
    KK = 3
    SHIFTS = (F + 1) // 2
    T1 = -(-SHIFTS // KK)
    R1 = F * KK
    A1 = 4
    SETS = F // 4
    REST = F - 4 * SETS
    SP3 = 3
    LOADS = SETS // SP3
    STEPS = SETS + 1
    PER = 2 + STEPS
    J = P // D
    U = P // J
    UG = U // GRP
    FB = F + 1
    H1, H2 = W_top1.shape[1], W_top2.shape[1]
    M1, M2 = H1 // P, H2 // P
    DC = dense_ctx.shape[1]
    LASTC = CHUNKS - 1

    x0_twice = nc.dram_tensor("x0_twice", [CHUNKS, GRP, 2 * F, N], fp32).ap()
    x0_by_set = nc.dram_tensor("x0_by_set", [CHUNKS, GRP, 4, SETS, N], fp32).ap()
    f0_fg = nc.dram_tensor("f0_fg", [F, 2 * F, M], fp32).ap()
    f0_gf = nc.dram_tensor("f0_gf", [F, 2 * F, M], fp32).ap()

    with ExitStack() as ctx:
        def sb(name, shape, dt=fp32):
            return ctx.enter_context(nc.sbuf_tensor(name, shape, dt))

        def ps(name, shape):
            return ctx.enter_context(nc.psum_tensor(name, shape, fp32))

        def sem(name):
            return ctx.enter_context(nc.semaphore(name))

        w1 = sb("w1", [R1, T1, M])
        w2 = sb("w2", [P, SETS, 4, M])
        w2_rest = sb("w2_rest", [P, REST, M])
        w3 = sb("w3", [P, F, M])
        wt1 = sb("wt1", [P, 3, H1])
        wt1_dense = sb("wt1_dense", [DC, H1])
        wt2 = sb("wt2", [P, M1, H2])
        wt3 = sb("wt3", [P, M2])
        bt1 = sb("bt1", [P, M1])
        bt2 = sb("bt2", [P, M2])
        ident = sb("ident", [P, P])
        own_sample = sb("own_sample", [P, J])
        own_shift = sb("own_shift", [R1, KK])
        keep = sb("keep", [R1, KK])
        ids_sb = sb("ids_sb", [P, CHUNKS, F], mybir.dt.int32)
        emb = sb("emb", [P, F, D])
        dense_T = sb("dense_T", [DC, B])
        x0T = sb("x0T", [F, D * P])
        pair_a = sb("pair_a", [R1, N])
        pair_b = sb("pair_b", [R1, T1, N])
        x0_set = sb("x0_set", [P, 2, SP3, N])
        x0_rest = sb("x0_rest", [P, REST, N])
        x1 = sb("x1", [P, 2, N])
        x1_rep = sb("x1_rep", [P, 2, 4, N])
        prod = sb("prod", [P, 2, 4, N])
        r1_part = sb("r1_part", [P, U, J])
        r1 = sb("r1", [P, P])
        x2 = sb("x2", [P, U, P])
        x2T = sb("x2T", [P, U, P])
        x0R = sb("x0R", [P, U, FB])
        x0_diag = sb("x0_diag", [P, U, J, FB])
        cross = sb("cross", [P, P, FB])
        r3 = sb("r3", [P, P])
        h1 = sb("h1", [P, M1, P])
        h2 = sb("h2", [P, M2, P])
        y_sb = sb("y_sb", [1, P])
        f0_sb = prod[0:R1, 0, 0:4, :].rearrange("p a n -> p (a n)")[:, 0:T1 * M].rearrange("p (c m) -> p c m", m=M)
        f0T_sb = prod[0:R1, 1, 0:4, :].rearrange("p a n -> p (a n)")[:, 0:T1 * M].rearrange("p (c m) -> p c m", m=M)
        dense_sb = x2T[:, 0, :].rearrange("p (c k) -> p c k", k=DC)

        p_x1 = ps("p_x1", [P, N])
        p_x2 = [ps(f"p_x2_{i}", [P, N]) for i in range(2)]
        p_tr = [ps(f"p_tr_{i}", [P, N]) for i in range(2)]
        p_cross = [ps(f"p_cross_{i}", [P, N]) for i in range(2)]
        p_top = ps("p_top", [P, N])

        filter1_copied = sem("filter1_copied")
        filter1_in = sem("filter1_in")
        filter2_in = sem("filter2_in")
        filter3_in = sem("filter3_in")
        top_in = sem("top_in")
        dense_in = sem("dense_in")
        ids_in = sem("ids_in")
        gathered = sem("gathered")
        ident_ready = sem("ident_ready")
        setup_done = sem("setup_done")
        ones_set = sem("ones_set")
        x0_stored = [sem(f"x0_stored_{g}") for g in range(GRP)]
        pairs_in = sem("pairs_in")
        sets_in = [sem(f"sets_in_{i}") for i in range(2)]
        rest_in = sem("rest_in")
        rep_in = [sem(f"rep_in_{i}") for i in range(2)]
        prod_ready = sem("prod_ready")
        prod_used = sem("prod_used")
        x1_ready = sem("x1_ready")
        x2_ready = sem("x2_ready")
        parts_ready = sem("parts_ready")
        r1_ready = sem("r1_ready")
        tr_ready = sem("tr_ready")
        tr_evac = sem("tr_evac")
        diag_ready = sem("diag_ready")
        cross_summed = sem("cross_summed")
        cross_ready = sem("cross_ready")
        top_summed = sem("top_summed")
        top_evac = sem("top_evac")
        out_stored = sem("out_stored")

        def is_last(c, g):
            return isinstance(c, int) and c == LASTC and g == GRP - 1

        def slot_at(c, g, j):
            return GRP * PER * c + PER * g + 2 + j - (2 if is_last(c, g) else 0)

        def layer1_slot(c, g, half):
            if g == 0:
                if isinstance(c, int) and c == 0:
                    return half
                return slot_at(c - 1, GRP - 1, half)
            return slot_at(c, g - 1, half)

        def group(c, g):
            return GRP * c + g

        def after(c, g):
            return (c, g + 1) if g + 1 < GRP else (c + 1, 0)

        def before(c, g):
            return (c, g - 1) if g else (c - 1, GRP - 1)

        def tr_x2T(c, k):
            if isinstance(c, int) and c == LASTC:
                return 12 + 10 * (c - 1) + 4 + k
            return 12 + 10 * c + k

        def tr_x0T(c, k):
            if isinstance(c, int) and c <= 1:
                return 6 * c + k
            return 12 + 10 * (c - 2) + 4 + k

        def tr_x0R(c, k):
            if isinstance(c, int) and c <= 1:
                return 6 * c + 4 + k
            return 12 + 10 * (c - 2) + 8 + k

        def top_use(c, k):
            return 2 + 4 * c + k

        def wait(eng, semaphore, count):
            if not (isinstance(count, int) and count <= 0):
                eng.wait_ge(semaphore, value(count))

        def worked_out(eng, count):
            return count if isinstance(count, int) else eng.snap(eng.to_reg(value(count)))

        def chunks(eng, body, end):
            body(0)
            with eng.Fori(0, LASTC - 1) as before_c:
                body(Linear(before_c, 1, 1))
            body(LASTC)
            if end:
                end()

        block = ctx.enter_context(nc.Block())

        @block.sync
        def _(sp):
            sp.dma_start(ids_sb[:], ids.rearrange("(c p) f -> p c f", p=P)).then_inc(ids_in, 16)
            sp.dma_start(f0_fg[:, 0:F, :], f0.rearrange("(f g) m -> f g m", g=F)).then_inc(filter1_copied, 16)
            sp.dma_start(f0_fg[:, F:2 * F, :], f0.rearrange("(f g) m -> f g m", g=F)).then_inc(filter1_copied, 16)
            sp.dma_start(f0_gf[:, 0:F, :], f0.rearrange("(f g) m -> g f m", g=F)).then_inc(filter1_copied, 16)
            sp.dma_start(f0_gf[:, F:2 * F, :], f0.rearrange("(f g) m -> g f m", g=F)).then_inc(filter1_copied, 16)
            sp.dma_start(dense_sb, dense_ctx.rearrange("(c p) k -> p c k", p=P)).then_inc(dense_in, 16)
            sp.wait_ge(filter1_copied, 64)
            for dst, src in ((f0_sb, f0_fg), (f0T_sb, f0_gf)):
                sp.dma_start(dst, AP(tensor=src.tensor, offset=0,
                                     ap=[[(2 * F + 1) * M, F], [T1 * M, KK], [1, T1 * M]])).then_inc(filter1_in, 16)

            def first_group(c, g):
                return isinstance(c, int) and c == 0 and g == 0

            def load_pairs(c, g):
                base = value((c * GRP + g) * (2 * F * N))
                stored = worked_out(sp, 48 * (c + 1))
                used = 0 if first_group(c, g) else worked_out(sp, layer1_slot(*before(c, g), 1) + 1)
                sp.wait_ge(x0_stored[g], stored)
                if not first_group(c, g):
                    sp.wait_ge(prod_ready, used)
                sp.dma_start(pair_a[:], AP(tensor=x0_twice.tensor, offset=base,
                                           ap=[[N, F], [0, KK], [1, N]])).then_inc(pairs_in, 16)
                sp.dma_start(pair_b[:].rearrange("p c n -> p (c n)"),
                             AP(tensor=x0_twice.tensor, offset=base,
                                ap=[[N, F], [T1 * N, KK], [1, T1 * N]])).then_inc(pairs_in, 16)

            def load_set(c, g, k):
                d = LOADS * g + k
                base = value((c * GRP + g) * (4 * SETS * N) + SP3 * k * N)
                if not (isinstance(c, int) and c == 0 and d < 2):
                    pc, pd = (c, d - 2) if d >= 2 else (c - 1, d - 2 + LOADS * GRP)
                    used = worked_out(sp, slot_at(pc, pd // LOADS, 2 + SP3 * (pd % LOADS) + SP3 - 1) + 1)
                    sp.wait_ge(prod_ready, used)
                sp.dma_start(x0_set[:, d % 2, :, :].rearrange("p s n -> p (s n)"),
                             AP(tensor=x0_by_set.tensor, offset=base,
                                ap=[[0, P // 4], [SETS * N, 4], [1, SP3 * N]])).then_inc(sets_in[d % 2], 16)

            def load_rest(c, g):
                base = value((c * GRP + g) * (2 * F * N) + 4 * SETS * N)
                if not first_group(c, g):
                    used = worked_out(sp, slot_at(*before(c, g), 2 + SETS) + 1)
                    sp.wait_ge(prod_ready, used)
                sp.dma_start(x0_rest[:].rearrange("p s n -> p (s n)"),
                             AP(tensor=x0_twice.tensor, offset=base,
                                ap=[[0, P], [1, REST * N]])).then_inc(rest_in, 16)

            def replicate(c, g):
                there = worked_out(sp, group(c, g) + 1)
                if not (isinstance(c, int) and group(c, g) < 2):
                    used = worked_out(sp, slot_at(*before(*before(c, g)), 1 + SETS) + 1)
                    sp.wait_ge(prod_ready, used)
                sp.wait_ge(x1_ready, there)
                for q in range(4):
                    rows = x1[q:P:4, g % 2, :]
                    sp.dma_start(x1_rep[:, g % 2, q, :],
                                 AP(tensor=rows.tensor, offset=rows.offset,
                                    ap=[list(rows.ap[0]), [0, 4], [1, N]])).then_inc(rep_in[g % 2], 16)

            load_pairs(0, 0)
            load_set(0, 0, 0)
            load_set(0, 0, 1)
            load_rest(0, 0)
            for s in range(SETS):
                sp.dma_start(w2[:, s, :, :].rearrange("p q m -> p (q m)"),
                             AP(tensor=f1.tensor, offset=4 * s * M * M,
                                ap=[[4 * M, P // 4], [M * M, 4], [1, 4 * M]])).then_inc(filter2_in, 16)
            sp.dma_start(w2_rest[:], AP(tensor=f1.tensor, offset=4 * SETS * M * M,
                                        ap=[[M, P], [M * M, REST], [1, M]])).then_inc(filter2_in, 16)
            replicate(0, 0)
            load_pairs(0, 1)

            def body(c):
                for g in range(GRP):
                    if not is_last(c, g):
                        replicate(*after(c, g))
                    two_on = after(*after(c, g))
                    if not (isinstance(two_on[0], int) and two_on[0] >= CHUNKS):
                        load_pairs(*two_on)
                    load_set(c, g, 2)
                    if isinstance(c, int) and c == 0 and g == 0:
                        sp.dma_start(w3[:], AP(tensor=f2.tensor, offset=0,
                                               ap=[[M, P], [M * M, F], [1, M]])).then_inc(filter3_in, 16)
                        sp.dma_start(wt1[:], W_top1[0:3 * P, :].rearrange("(k p) n -> p k n", p=P)).then_inc(top_in, 16)
                        sp.dma_start(wt1_dense[:], W_top1[3 * P:3 * P + DC, :]).then_inc(top_in, 16)
                        sp.dma_start(wt2[:], W_top2.rearrange("(k p) n -> p k n", p=P)).then_inc(top_in, 16)
                        sp.dma_start(wt3[:], W_top3.rearrange("(k p) n -> p (k n)", p=P),
                                     allow_slow_non_contiguous=True).then_inc(top_in, 16)
                        sp.dma_start(bt1[:], b_top1.rearrange("(k p) -> p k", p=P),
                                     allow_slow_non_contiguous=True).then_inc(top_in, 16)
                        sp.dma_start(bt2[:], b_top2.rearrange("(k p) -> p k", p=P),
                                     allow_slow_non_contiguous=True).then_inc(top_in, 16)
                    if not is_last(c, g):
                        nxt = after(c, g)
                        load_set(*nxt, 0)
                        load_set(*nxt, 1)
                        load_rest(*nxt)

            chunks(sp, body, None)
            sp.wait_ge(out_stored, 16 * CHUNKS)

        @block.gpsimd
        def _(pool):
            pool.memset(ident[:], 0.0).then_inc(ident_ready, 1)
            pool.wait_ge(ident_ready, 1)
            pool.affine_select(out=ident[:], in_=ident[:], compare_op=ALU.not_equal, fill=1.0, base=0,
                               pattern=[[-1, P]], channel_multiplier=1).then_inc(ident_ready, 1)
            pool.wait_ge(ids_in, 16)
            for c in range(CHUNKS):
                if c:
                    pool.wait_ge(tr_ready, tr_x0T(c - 1, GRP - 1) + 1)
                for f in range(F):
                    pool.indirect_dma_start(emb[:, f, :], None, tables[f],
                                            bass.IndirectOffsetOnAxis(ap=ids_sb[:, c, f:f + 1], axis=0)
                                            ).then_inc(gathered, 16)

        @block.vector
        def _(dve):
            dve.memset(x0R[:, :, F:FB], 1.0).then_inc(ones_set, 1)
            dve.wait_ge(ident_ready, 2)
            dve.reduce_sum(own_sample[:], ident[:].rearrange("p (d j) -> p j d", j=J), AX.X).then_inc(setup_done, 1)
            dve.reduce_sum(own_shift[:], ident[0:R1, 0:R1].rearrange("p (f k) -> p k f", k=KK),
                           AX.X).then_inc(setup_done, 1)
            dve.wait_ge(setup_done, 2)
            dve.tensor_scalar(keep[:], own_shift[:], -1.0, 1.0, ALU.mult, ALU.add).then_inc(setup_done, 1)
            dve.wait_ge(filter1_in, 32)
            dve.wait_ge(setup_done, 3)
            dve.tensor_scalar(f0T_sb[:, 0, :], f0T_sb[:, 0, :], keep[:, 0:1], None, ALU.mult).then_inc(setup_done, 1)
            dve.wait_ge(setup_done, 4)
            dve.tensor_tensor(w1[:], f0_sb, f0T_sb, ALU.add).then_inc(setup_done, 1)
            dve.wait_ge(setup_done, 5)
            dve.tensor_scalar(w1[:, T1 - 1, :], w1[:, T1 - 1, :], keep[:, KK - 1:KK], None,
                              ALU.mult).then_inc(setup_done, 1)
            dve.wait_ge(setup_done, 6)

            def slot_free(n):
                wait(dve, prod_used, n - 1)

            def layer1(c, g):
                dve.wait_ge(pairs_in, value(32 * (group(c, g) + 1)))
                for half, lo, hi in ((0, 0, A1), (1, A1, T1)):
                    slot_free(layer1_slot(c, g, half))
                    a = pair_a[:].unsqueeze(1).broadcast_to([R1, hi - lo, N])
                    dve.tensor_tensor(prod[0:R1, half, 0:hi - lo, :], pair_b[:, lo:hi, :], a,
                                      ALU.mult).then_inc(prod_ready, 1)

            def part(c, g):
                dve.wait_ge(x1_ready, value(group(c, g) + 1))
                dve.reduce_sum(r1_part[:, UG * g:UG * (g + 1), :],
                               x1[:, g % 2, :].rearrange("p (u d j) -> p u j d", d=D, j=J),
                               AX.X).then_inc(parts_ready, 1)

            layer1(0, 0)
            part(0, 0)

            def body(c):
                for g in range(GRP):
                    if not is_last(c, g):
                        layer1(*after(c, g))
                    for s in range(SETS):
                        d = LOADS * g + s // SP3
                        if s == 0:
                            dve.wait_ge(rep_in[g % 2], value(64 * (2 * c + g // 2 + 1)))
                        if s % SP3 == 0:
                            dve.wait_ge(sets_in[d % 2], value(16 * ((LOADS * GRP // 2) * c + d // 2 + 1)))
                        n = slot_at(c, g, 2 + s)
                        slot_free(n)
                        x0b = x0_set[:, d % 2, s % SP3, :].unsqueeze(1).broadcast_to([P, 4, N])
                        dve.tensor_tensor(prod[:, s % 2, :, :], x1_rep[:, g % 2, :, :], x0b,
                                          ALU.mult).then_inc(prod_ready, 1)
                    dve.wait_ge(rest_in, value(16 * (group(c, g) + 1)))
                    n = slot_at(c, g, 2 + SETS)
                    slot_free(n)
                    x1b = x1[:, g % 2, :].unsqueeze(1).broadcast_to([P, REST, N])
                    dve.tensor_tensor(prod[:, SETS % 2, 0:REST, :], x0_rest[:], x1b, ALU.mult).then_inc(prod_ready, 1)
                    if g == GRP - 1:
                        dve.wait_ge(parts_ready, value(GRP * (c + 1)))
                        wait(dve, top_summed, top_use(c - 1, 1) + 1 if not (isinstance(c, int) and c == 0) else 0)
                        dve.tensor_copy(r1[:], r1_part[:].rearrange("p u j -> p (u j)")).then_inc(r1_ready, 1)
                        dve.wait_ge(r1_ready, value(c + 1))
                    if not is_last(c, g):
                        part(*after(c, g))

            chunks(dve, body, None)

        @block.scalar
        def _(act):
            def evac(dst, idx, src):
                act.wait_ge(tr_ready, value(idx + 1))
                act.activation(dst, src, ACT.Copy).then_inc(tr_evac, 1)

            def x0T_batch(c, k):
                if k == 0 and not (isinstance(c, int) and c == 0):
                    for g in range(GRP):
                        act.wait_ge(x0_stored[g], value(48 * c))
                evac(x0T[:].rearrange("f (u d j) -> f d u j", d=D, j=J)[:, DB * k:DB * (k + 1)], tr_x0T(c, k),
                     p_tr[k % 2][0:F, :].rearrange("f (d u j) -> f d u j", u=U, j=J))

            def x0_store(c, g):
                act.wait_ge(tr_evac, value(tr_x0T(c, GRP - 1) + 1))
                cols = slice(g * N, (g + 1) * N)
                base = (c * GRP + g) * (2 * F * N)
                for half in range(2):
                    act.dma_start(AP(tensor=x0_twice.tensor, offset=value(base + half * F * N), ap=[[N, F], [1, N]]),
                                  x0T[:, cols]).then_inc(x0_stored[g], 16)
                act.dma_start(AP(tensor=x0_by_set.tensor, offset=value((c * GRP + g) * (4 * SETS * N)),
                                 ap=[[N, SETS], [SETS * N, 4], [1, N]]),
                              x0T[0:4 * SETS, cols]).then_inc(x0_stored[g], 16)

            def x0R_batch(c, k):
                if not (isinstance(c, int) and c == 0):
                    act.wait_ge(diag_ready, value(J * c))
                evac(x0R[:, 8 * k:8 * k + 8, 0:F], tr_x0R(c, k),
                     p_tr[k % 2][:, 0:8 * FB].rearrange("p (u f) -> p u f", f=FB)[:, :, 0:F])

            def x1_out(c, g):
                act.wait_ge(prod_used, value(layer1_slot(c, g, 1) + 1))
                if not (isinstance(c, int) and group(c, g) < 2):
                    b2 = before(*before(c, g))
                    act.wait_ge(prod_ready, value(slot_at(*b2, 2 + SETS) + 1))
                    act.wait_ge(parts_ready, value(group(*b2) + 1))
                    act.wait_ge(rep_in[g % 2], value(64 * (2 * b2[0] + b2[1] // 2 + 1)))
                act.activation(x1[:, g % 2, :], p_x1[:], ACT.Copy).then_inc(x1_ready, 1)

            def x2_out(c, g):
                act.wait_ge(prod_used, value(slot_at(c, g, 1 + STEPS) + 1))
                if not (isinstance(c, int) and c == 0) and g == 0:
                    act.wait_ge(tr_ready, value(tr_x2T(c - 1, 3) + 1))
                act.activation(x2[:, UG * g:UG * (g + 1), :].rearrange("p u n -> p (u n)"), p_x2[g % 2][:],
                               ACT.Copy).then_inc(x2_ready, 1)

            def x2T_out(c):
                for k in range(4):
                    evac(x2T[:, 4 * k:4 * k + 4, :].rearrange("p u m -> p (u m)"), tr_x2T(c, k), p_tr[k % 2][:])

            def diag(c):
                act.wait_ge(tr_evac, value(tr_x0R(c, 1) + 1))
                for j in range(J):
                    act.activation(x0_diag[:, :, j, :], x0R[:], ACT.Copy,
                                   scale=own_sample[:, j:j + 1]).then_inc(diag_ready, 1)

            def cross_out(c):
                for u in range(U):
                    act.wait_ge(cross_summed, value(U * c + u + 1))
                    act.activation(cross[:, J * u:J * (u + 1), :].rearrange("p b f -> p (b f)"),
                                   p_cross[u % 2][:, 0:J * FB], ACT.Copy).then_inc(cross_ready, 1)

            def r3_out(c):
                act.wait_ge(top_summed, value(top_use(c, 0) + 1))
                act.activation(r3[:], p_top[:, 0:P], ACT.Copy).then_inc(top_evac, 1)

            def h1_out(c):
                act.wait_ge(top_summed, value(top_use(c, 1) + 1))
                for m in range(M1):
                    last = act.activation(h1[:, m, :], p_top[:, m * P:(m + 1) * P], ACT.Relu, bias=bt1[:, m:m + 1])
                last.then_inc(top_evac, 1)

            def h2_out(c):
                act.wait_ge(top_summed, value(top_use(c, 2) + 1))
                for m in range(M2):
                    last = act.activation(h2[:, m, :], p_top[:, m * P:(m + 1) * P], ACT.Relu, bias=bt2[:, m:m + 1])
                last.then_inc(top_evac, 1)

            def y_out(c):
                act.wait_ge(top_summed, value(top_use(c, 3) + 1))
                act.activation(y_sb[:], p_top[0:1, 0:P], ACT.Copy).then_inc(top_evac, 1)
                act.wait_ge(top_evac, value(top_use(c, 3) + 1))
                act.dma_start(AP(tensor=out.tensor, offset=value(c * P), ap=[[P, 1], [1, P]]), y_sb[:]).then_inc(out_stored, 16)

            act.wait_ge(ones_set, 1)
            act.wait_ge(setup_done, 1)
            for k in range(GRP):
                x0T_batch(0, k)
            for g in range(GRP):
                x0_store(0, g)
            for k in range(2):
                x0R_batch(0, k)
            for k in range(2):
                act.wait_ge(top_summed, k + 1)
                act.activation(dense_T[:, k * N:(k + 1) * N], p_top[0:DC, :], ACT.Copy).then_inc(top_evac, 1)
            x1_out(0, 0)

            def body(c):
                first = isinstance(c, int) and c == 0
                final = isinstance(c, int) and c == LASTC
                for g in range(GRP):
                    if not is_last(c, g):
                        x1_out(*after(c, g))
                    if g == 0:
                        if not first:
                            x2T_out(c - 1)
                        if not final:
                            for k in range(GRP):
                                x0T_batch(c + 1, k)
                            for k in range(GRP):
                                x0_store(c + 1, k)
                    if g == 1 and not first:
                        cross_out(c - 1)
                    if g == 2:
                        diag(c)
                        if not first:
                            r3_out(c - 1)
                    if g == 3:
                        if not first:
                            if isinstance(c, int) and c == 1 or not isinstance(c, int):
                                act.wait_ge(top_in, 96)
                            h1_out(c - 1)
                        if not final:
                            for k in range(2):
                                x0R_batch(c + 1, k)
                        if not first:
                            h2_out(c - 1)
                            y_out(c - 1)
                    x2_out(c, g)
                if not first:
                    act.wait_ge(out_stored, value(16 * c))

            def end():
                x2T_out(LASTC)
                cross_out(LASTC)
                r3_out(LASTC)
                h1_out(LASTC)
                h2_out(LASTC)
                y_out(LASTC)

            chunks(act, body, end)

        @block.tensor
        def _(pe):
            def bank_free(idx):
                wait(pe, tr_evac, idx - 1)

            def x0T_waits(c, k):
                if k == 0:
                    pe.wait_ge(gathered, value(16 * F * (c + 1)))
                bank_free(tr_x0T(c, k))

            def x0T_batch(c, k):
                for i in range(DB):
                    last = pe.transpose(p_tr[k % 2][0:F, i * P:(i + 1) * P], emb[:, :, DB * k + i], ident[:])
                last.then_inc(tr_ready, 1)

            def x0R_waits(c, k):
                pe.wait_ge(tr_evac, value(tr_x0T(c, GRP - 1) + 1))
                bank_free(tr_x0R(c, k))

            def x0R_batch(c, k):
                for i in range(8):
                    u = 8 * k + i
                    last = pe.transpose(p_tr[k % 2][:, i * FB:i * FB + F], x0T[:, u * P:(u + 1) * P],
                                        ident[0:F, 0:F])
                last.then_inc(tr_ready, 1)

            def x2T_batch(c, k):
                pe.wait_ge(x2_ready, value(GRP * (c + 1)))
                bank_free(tr_x2T(c, k))
                for i in range(4):
                    u = 4 * k + i
                    last = pe.transpose(p_tr[k % 2][:, i * P:(i + 1) * P], x2[:, u, :], ident[:])
                last.then_inc(tr_ready, 1)

            def contract(c, u):
                if u == 0:
                    pe.wait_ge(tr_evac, value(tr_x2T(c, 3) + 1))
                    pe.wait_ge(diag_ready, value(J * (c + 1)))
                if u >= 2:
                    pe.wait_ge(cross_ready, value(U * c + u - 1))
                pe.matmul(p_cross[u % 2][:, 0:J * FB], x2T[:, u, :],
                          x0_diag[:, u, :, :].rearrange("p j f -> p (j f)"),
                          start=True, stop=True).then_inc(cross_summed, 1)

            def layer3(c, fields):
                for f in fields:
                    if f == 0:
                        pe.wait_ge(cross_ready, value(U * (c + 1)))
                        pe.wait_ge(filter3_in, 16)
                        pe.wait_ge(top_evac, value(top_use(c, 0)))
                    last = pe.matmul(p_top[:, 0:P], w3[:, f, :], cross[:, :, f], start=(f == 0), stop=(f == F - 1))
                    if f == F - 1:
                        last.then_inc(top_summed, 1)

            def top1(c):
                pe.wait_ge(top_evac, value(top_use(c, 1)))
                pe.wait_ge(r1_ready, value(c + 1))
                pe.wait_ge(top_in, 96)
                for m in range(M1):
                    cols = slice(m * P, (m + 1) * P)
                    pe.matmul(p_top[:, cols], wt1[:, 0, cols], r1[:], start=True, stop=False)
                    pe.matmul(p_top[:, cols], wt1[:, 1, cols], cross[:, :, F], start=False, stop=False)
                    pe.matmul(p_top[:, cols], wt1[:, 2, cols], r3[:], start=False, stop=False)
                    last = pe.matmul(p_top[:, cols], wt1_dense[:, cols], dense_T[:, bass.ds(value(c * P), P)],
                                     start=False, stop=True)
                last.then_inc(top_summed, 1)

            def top2(c):
                pe.wait_ge(top_evac, value(top_use(c, 2)))
                for m in range(M2):
                    for k in range(M1):
                        last = pe.matmul(p_top[:, m * P:(m + 1) * P], wt2[:, k, m * P:(m + 1) * P], h1[:, k, :],
                                         start=(k == 0), stop=(k == M1 - 1))
                last.then_inc(top_summed, 1)

            def top3(c):
                pe.wait_ge(top_evac, value(top_use(c, 3)))
                for k in range(M2):
                    last = pe.matmul(p_top[0:1, 0:P], wt3[:, k:k + 1], h2[:, k, :], start=(k == 0), stop=(k == M2 - 1))
                last.then_inc(top_summed, 1)

            def layer1(c, g):
                for half, lo, hi in ((0, 0, A1), (1, A1, T1)):
                    pe.wait_ge(prod_ready, value(layer1_slot(c, g, half) + 1))
                    if half == 0:
                        wait(pe, x1_ready, group(c, g))
                    for t in range(lo, hi):
                        last = pe.matmul(p_x1[:], w1[:, t, :], prod[0:R1, half, t - lo, :],
                                         start=(t == 0), stop=(t == T1 - 1))
                    last.then_inc(prod_used, 1)

            def ahead(c, g, s):
                if isinstance(c, int) and c == LASTC:
                    return
                if g == 0 and 5 <= s <= 8:
                    x0T_waits(c + 1, s - 5)
                if g == 3 and s in (3, 4):
                    x0R_waits(c + 1, s - 3)

            def between(c, g, s):
                first = isinstance(c, int) and c == 0
                final = isinstance(c, int) and c == LASTC
                if g == 0 and 1 <= s <= 4 and not first:
                    x2T_batch(c - 1, s - 1)
                if g == 0 and 5 <= s <= 8 and not final:
                    x0T_batch(c + 1, s - 5)
                if g == 1 and s < 8 and not first:
                    contract(c - 1, 2 * s)
                    contract(c - 1, 2 * s + 1)
                if g == 2 and not first:
                    layer3(c - 1, range(4 * s, min(4 * s + 4, F)))
                if g == 3:
                    if s == 1 and not first:
                        top1(c - 1)
                    if s in (3, 4) and not final:
                        x0R_batch(c + 1, s - 3)
                    if s == 6 and not first:
                        top2(c - 1)
                    if s == 8 and not first:
                        top3(c - 1)

            def layer2(c, g):
                bank = p_x2[g % 2]
                for s in range(STEPS):
                    pe.wait_ge(prod_ready, value(slot_at(c, g, 2 + s) + 1))
                    if s == 0:
                        wait(pe, x2_ready, group(c, g) - 1)
                    tiles = 4 if s < SETS else REST
                    for q in range(tiles):
                        if q == tiles - 1:
                            ahead(c, g, s)
                        weights = w2[:, s, q, :] if s < SETS else w2_rest[:, q, :]
                        last = pe.matmul(bank[:], weights, prod[:, s % 2, q, :],
                                         start=(s == 0 and q == 0), stop=(s == STEPS - 1 and q == tiles - 1))
                    last.then_inc(prod_used, 1)
                    between(c, g, s)

            pe.wait_ge(ident_ready, 2)
            for k in range(GRP):
                x0T_waits(0, k)
                x0T_batch(0, k)
            for k in range(2):
                x0R_waits(0, k)
                x0R_batch(0, k)
            pe.wait_ge(dense_in, 16)
            for k in range(2):
                wait(pe, top_evac, k)
                for i in range(4):
                    last = pe.transpose(p_top[0:DC, i * P:(i + 1) * P], dense_sb[:, 4 * k + i, :], ident[:])
                last.then_inc(top_summed, 1)
            pe.wait_ge(setup_done, 6)
            layer1(0, 0)
            pe.wait_ge(filter2_in, 16 * (SETS + 1))

            def body(c):
                for g in range(GRP):
                    if not is_last(c, g):
                        layer1(*after(c, g))
                    layer2(c, g)

            def end():
                for k in range(4):
                    x2T_batch(LASTC, k)
                for u in range(U):
                    contract(LASTC, u)
                layer3(LASTC, range(F))
                top1(LASTC)
                top2(LASTC)
                top3(LASTC)

            chunks(pe, body, end)


def kernel(**inputs):
    import numpy as np
    import concourse.bacc as bacc
    from concourse.bass_utils import run_bass_kernel_spmd

    nc = bacc.Bacc("TRN2", target_bir_lowering=False, num_devices=1)
    arrays, handles = {}, {}
    for name, value in inputs.items():
        a = np.ascontiguousarray(value)
        arrays[f"in_{name}"] = a
        handles[name] = nc.dram_tensor(f"in_{name}", a.shape, mybir.dt.from_np(a.dtype), kind="ExternalInput").ap()
    batch, fields = inputs["ids"].shape
    out = nc.dram_tensor("out", (batch, 1), mybir.dt.float32, kind="ExternalOutput").ap()
    build_cin_tower(nc, handles["dense_ctx"], handles["ids"], [handles[f"tbl_{f}"] for f in range(fields)],
                    handles["W_top1"], handles["b_top1"], handles["W_top2"], handles["b_top2"], handles["W_top3"],
                    handles["L0_rec_f0"], handles["L0_rec_f1"], handles["L0_rec_f2"], out)
    r = run_bass_kernel_spmd(nc, [arrays], core_ids=[0])
    return r.results[0]["out"]
```

```python
import concourse.bass as bass
from concourse import mybir
from contextlib import ExitStack


class Linear:

    def __init__(self, register, times, plus):
        self.register, self.times, self.plus = register, times, plus

    def __add__(self, k):
        return Linear(self.register, self.times, self.plus + k)

    def __sub__(self, k):
        return self + -k

    def __mul__(self, k):
        return Linear(self.register, self.times * k, self.plus * k)

    __radd__, __rmul__ = __add__, __mul__


def value(x):
    return x if isinstance(x, int) else x.register * x.times + x.plus


def build_cin_tower(nc, dense_ctx, ids, tables, W_top1, b_top1, W_top2, b_top2, W_top3, f0, f1, f2, out):
    fp32 = mybir.dt.float32
    fp32r = mybir.dt.float32r
    ALU = mybir.AluOpType
    ACT = mybir.ActivationFunctionType
    AX = mybir.AxisListType
    AP = bass.AP

    B, F = ids.shape
    D = tables[0].shape[1]
    M = f0.shape[1]
    P = 128
    CHUNKS = B // P
    GRP = 4
    DB = D // GRP
    N = P // GRP * D
    GROUPS = CHUNKS * GRP
    KK = 3
    SHIFTS = (F + 1) // 2
    T1 = -(-SHIFTS // KK)
    R1 = F * KK
    STEP1 = ((0, 4), (4, T1))
    SPLIT = 2
    SETS = F // 4
    REST = F - 4 * SETS
    SETBUFS = 4
    STEPS = 1 + SETS
    PER = 2 + STEPS
    SRING, NRING = 3, 3
    LAG = 2
    J = P // D
    U = P // J
    UG = U // GRP
    FB = F + 1
    H1, H2 = W_top1.shape[1], W_top2.shape[1]
    M1, M2 = H1 // P, H2 // P
    DC = dense_ctx.shape[1]
    LASTC = CHUNKS - 1
    X2T_AT = (1, 21, 33, 39)
    CONTRACT_AT = ((3, 4, 5, 6), (26, 27, 30, 31), (35, 36, 37, 38), (42, 43, 44, 45))
    X0T_AT, X0R_AT = (7, 18, 19, 20), (46, 47)
    L3_FIELDS = 4
    L3_AT = tuple(range(8, 8 + -(-F // L3_FIELDS)))
    TOP1_AT, TOP2_AT, TOP3_AT = (22, 23, 24, 25), (28, 29), 32
    DIAG_AT = ((9, 10), (31, 32), (38, 39), (45, 46))

    x0_twice = nc.dram_tensor("x0_twice", [CHUNKS, GRP, 2 * F, N], fp32).ap()
    x0_by_set = nc.dram_tensor("x0_by_set", [CHUNKS, GRP, 4, SETS, N], fp32).ap()
    f0_fg = nc.dram_tensor("f0_fg", [F, 2 * F, M], fp32).ap()
    f0_gf = nc.dram_tensor("f0_gf", [F, 2 * F, M], fp32).ap()

    with ExitStack() as ctx:
        def sb(name, shape, dt=fp32):
            return ctx.enter_context(nc.sbuf_tensor(name, shape, dt))

        def ps(name, shape):
            return ctx.enter_context(nc.psum_tensor(name, shape, fp32))

        def sem(name):
            return ctx.enter_context(nc.semaphore(name))

        w1_native = sb("w1_native", [R1, T1 - 2 * SPLIT, M])
        w1_high = sb("w1_high", [R1, 2 * SPLIT, M], fp32r)
        w1_low = sb("w1_low", [R1, 2 * SPLIT, M], fp32r)
        w2_native = sb("w2_native", [P, SETS, 4 - SPLIT, M])
        w2_high = sb("w2_high", [P, SETS, SPLIT, M], fp32r)
        w2_low = sb("w2_low", [P, SETS, SPLIT, M], fp32r)
        w2_rest = sb("w2_rest", [P, REST - SPLIT, M])
        w2_rest_high = sb("w2_rest_high", [P, SPLIT, M], fp32r)
        w2_rest_low = sb("w2_rest_low", [P, SPLIT, M], fp32r)
        w3 = sb("w3", [P, F, M])
        wt1 = sb("wt1", [P, 3, H1])
        wt1_dense = sb("wt1_dense", [DC, H1])
        wt2 = sb("wt2", [P, M1, H2])
        wt3 = sb("wt3", [P, M2])
        bt1 = sb("bt1", [P, M1])
        bt2 = sb("bt2", [P, M2])
        ident = sb("ident", [P, P])
        own_sample = sb("own_sample", [P, J])
        own_shift = sb("own_shift", [R1, KK])
        keep = sb("keep", [R1, KK])
        ids_sb = sb("ids_sb", [P, CHUNKS, F], mybir.dt.int32)
        emb = sb("emb", [P, F, D])
        dense_T = sb("dense_T", [DC, B])
        x0T = sb("x0T", [F, D * P])
        pair_a = sb("pair_a", [R1, N])
        pair_b = sb("pair_b", [R1, T1, N])
        x0_set = sb("x0_set", [P, SETBUFS, N])
        x0_rest = sb("x0_rest", [P, REST, N])
        x1 = sb("x1", [P, N])
        x1_rep = sb("x1_rep", [P, 2, 4, N])
        prod = sb("prod", [P, SPLIT * SRING + (4 - SPLIT) * NRING, N])
        prod_high = sb("prod_high", [P, 2, SPLIT, N], fp32r)
        prod_low = sb("prod_low", [P, 2, SPLIT, N], fp32r)
        r1_part = sb("r1_part", [P, U, J])
        r1 = sb("r1", [P, P])
        x2 = sb("x2", [P, UG, P])
        x2T = sb("x2T", [P, UG, P])
        x0R = sb("x0R", [P, U, FB])
        x0_diag = sb("x0_diag", [P, UG, J, FB])
        cross = sb("cross", [P, P, FB])
        r3 = sb("r3", [P, P])
        h1 = sb("h1", [P, M1, P])
        h2 = sb("h2", [P, M2, P])
        y_sb = sb("y_sb", [1, P])
        prod_flat = prod[:].rearrange("p a n -> p (a n)")
        f0_sb = prod_flat[0:R1, 0:T1 * M].rearrange("p (c m) -> p c m", m=M)
        f0T_sb = prod_flat[0:R1, T1 * M:2 * T1 * M].rearrange("p (c m) -> p c m", m=M)
        rep_flat = x1_rep[:].rearrange("p a q n -> p (a q n)")
        f1_split = rep_flat[:, 0:SETS * SPLIT * M].rearrange("p (s c m) -> p s c m", s=SETS, m=M)
        f1_rest = rep_flat[:, SETS * SPLIT * M:(SETS + 1) * SPLIT * M].rearrange("p (c m) -> p c m", m=M)
        dense_sb = x2T[:, 0, :].rearrange("p (c k) -> p c k", k=DC)

        p_x1 = ps("p_x1", [P, N])
        p_x2 = [ps(f"p_x2_{i}", [P, N]) for i in range(2)]
        p_tr = [ps(f"p_tr_{i}", [P, N]) for i in range(2)]
        p_cross = [ps(f"p_cross_{i}", [P, N]) for i in range(2)]
        p_top = ps("p_top", [P, N])

        filter1_copied = sem("filter1_copied")
        filter1_in = sem("filter1_in")
        filter2_in = sem("filter2_in")
        filter3_in = sem("filter3_in")
        top_in = sem("top_in")
        dense_in = sem("dense_in")
        ids_in = sem("ids_in")
        gathered = sem("gathered")
        ident_ready = sem("ident_ready")
        setup_done = sem("setup_done")
        ones_set = sem("ones_set")
        x0_stored = [sem(f"x0_stored_{g}") for g in range(GRP)]
        pairs_in = sem("pairs_in")
        sets_in = [sem(f"sets_in_{i}") for i in range(SETBUFS)]
        rest_in = sem("rest_in")
        rep_in = [sem(f"rep_in_{i}") for i in range(2)]
        weights_high = sem("weights_high")
        weights_split = sem("weights_split")
        prod_ready = sem("prod_ready")
        high_ready = sem("high_ready")
        low_ready = sem("low_ready")
        native_used = sem("native_used")
        split_used = sem("split_used")
        x1_ready = sem("x1_ready")
        x2_ready = sem("x2_ready")
        parts_ready = sem("parts_ready")
        r1_ready = sem("r1_ready")
        tr_ready = sem("tr_ready")
        tr_evac = sem("tr_evac")
        diag_ready = sem("diag_ready")
        cross_summed = sem("cross_summed")
        cross_ready = sem("cross_ready")
        top_summed = sem("top_summed")
        top_evac = sem("top_evac")
        out_stored = sem("out_stored")

        def is_last(c, g):
            return isinstance(c, int) and c == LASTC and g == GRP - 1

        def step_at(c, g, j):
            return GRP * PER * c + PER * g + 2 + j - (2 if is_last(c, g) else 0)

        def layer1_step(c, g, half):
            if g == 0:
                if isinstance(c, int) and c == 0:
                    return half
                return step_at(c - 1, GRP - 1, half)
            return step_at(c, g - 1, half)

        def group(c, g):
            return GRP * c + g

        def after(c, g):
            return (c, g + 1) if g + 1 < GRP else (c + 1, 0)

        def before(c, g):
            return (c, g - 1) if g else (c - 1, GRP - 1)

        def place(x, ring):
            if isinstance(x, int):
                return x % ring
            assert x.times % ring == 0
            return x.plus % ring

        def tr_x2T(c, g):
            if isinstance(c, int) and c == LASTC:
                return 5 + 10 * c + 1 + g
            return 5 + 10 * (c + 1) if g == GRP - 1 else 5 + 10 * c + 5 + g

        def tr_x0T(c, k):
            return k if isinstance(c, int) and c == 0 else 5 + 10 * (c - 1) + 1 + k

        def tr_x0R(c, k):
            return 4 + k if isinstance(c, int) and c == 0 else 5 + 10 * (c - 1) + 8 + k

        def top_use(c, k):
            return 2 + 4 * c + k

        def wait(eng, semaphore, count):
            if not (isinstance(count, int) and count <= 0):
                eng.wait_ge(semaphore, value(count))

        def worked_out(eng, count):
            return count if isinstance(count, int) else eng.snap(eng.to_reg(value(count)))

        def chunks(eng, body, end):
            body(0)
            with eng.Fori(0, LASTC - 1) as before_c:
                body(Linear(before_c, 1, 1))
            body(LASTC)
            if end:
                end()

        block = ctx.enter_context(nc.Block())

        @block.sync
        def _(sp):
            sp.dma_start(ids_sb[:], ids.rearrange("(c p) f -> p c f", p=P)).then_inc(ids_in, 16)
            sp.dma_start(f0_fg[:, 0:F, :], f0.rearrange("(f g) m -> f g m", g=F)).then_inc(filter1_copied, 16)
            sp.dma_start(f0_fg[:, F:2 * F, :], f0.rearrange("(f g) m -> f g m", g=F)).then_inc(filter1_copied, 16)
            sp.dma_start(f0_gf[:, 0:F, :], f0.rearrange("(f g) m -> g f m", g=F)).then_inc(filter1_copied, 16)
            sp.dma_start(f0_gf[:, F:2 * F, :], f0.rearrange("(f g) m -> g f m", g=F)).then_inc(filter1_copied, 16)
            sp.dma_start(dense_sb, dense_ctx.rearrange("(c p) k -> p c k", p=P)).then_inc(dense_in, 16)
            for s in range(SETS):
                for dst, q in ((f1_split[:, s], 0), (w2_native[:, s], SPLIT)):
                    sp.dma_start(dst.rearrange("p q m -> p (q m)"),
                                 AP(tensor=f1.tensor, offset=4 * s * M * M + q * M,
                                    ap=[[4 * M, P // 4], [M * M, 4], [1, 2 * M]])).then_inc(filter2_in, 16)
            for dst, f, n in ((f1_rest, 0, SPLIT), (w2_rest[:], SPLIT, REST - SPLIT)):
                sp.dma_start(dst, AP(tensor=f1.tensor, offset=(4 * SETS + f) * M * M,
                                     ap=[[M, P], [M * M, n], [1, M]])).then_inc(filter2_in, 16)
            sp.wait_ge(filter1_copied, 64)
            for dst, src in ((f0_sb, f0_fg), (f0T_sb, f0_gf)):
                sp.dma_start(dst, AP(tensor=src.tensor, offset=0,
                                     ap=[[(2 * F + 1) * M, F], [T1 * M, KK], [1, T1 * M]])).then_inc(filter1_in, 16)
            sp.dma_start(w3[:], AP(tensor=f2.tensor, offset=0,
                                   ap=[[M, P], [M * M, F], [1, M]])).then_inc(filter3_in, 16)
            sp.dma_start(wt1[:], W_top1[0:3 * P, :].rearrange("(k p) n -> p k n", p=P)).then_inc(top_in, 16)
            sp.dma_start(wt1_dense[:], W_top1[3 * P:3 * P + DC, :]).then_inc(top_in, 16)
            sp.dma_start(wt2[:], W_top2.rearrange("(k p) n -> p k n", p=P)).then_inc(top_in, 16)
            sp.dma_start(wt3[:], W_top3.rearrange("(k p) n -> p (k n)", p=P),
                         allow_slow_non_contiguous=True).then_inc(top_in, 16)
            sp.dma_start(bt1[:], b_top1.rearrange("(k p) -> p k", p=P),
                         allow_slow_non_contiguous=True).then_inc(top_in, 16)
            sp.dma_start(bt2[:], b_top2.rearrange("(k p) -> p k", p=P),
                         allow_slow_non_contiguous=True).then_inc(top_in, 16)

            def first_group(c, g):
                return isinstance(c, int) and c == 0 and g == 0

            def load_pairs(c, g):
                base = value((c * GRP + g) * (2 * F * N))
                stored = worked_out(sp, 32 * (c + 1))
                used = 0 if first_group(c, g) else worked_out(sp, layer1_step(*before(c, g), 1) + 1)
                sp.wait_ge(x0_stored[g], stored)
                if not first_group(c, g):
                    sp.wait_ge(prod_ready, used)
                sp.dma_start(pair_a[:], AP(tensor=x0_twice.tensor, offset=base,
                                           ap=[[N, F], [0, KK], [1, N]])).then_inc(pairs_in, 16)
                sp.dma_start(pair_b[:].rearrange("p c n -> p (c n)"),
                             AP(tensor=x0_twice.tensor, offset=base,
                                ap=[[N, F], [T1 * N, KK], [1, T1 * N]])).then_inc(pairs_in, 16)

            def load_set(c, g, s):
                d = SETS * g + s
                base = value((c * GRP + g) * (4 * SETS * N) + s * N)
                if not (isinstance(c, int) and c == 0 and d < SETBUFS):
                    pc, pd = (c, d - SETBUFS) if d >= SETBUFS else (c - 1, d - SETBUFS + SETS * GRP)
                    used = worked_out(sp, step_at(pc, pd // SETS, 3 + pd % SETS) + 1)
                    sp.wait_ge(prod_ready, used)
                sp.dma_start(x0_set[:, d % SETBUFS, :],
                             AP(tensor=x0_by_set.tensor, offset=base,
                                ap=[[0, P // 4], [SETS * N, 4], [1, N]])).then_inc(sets_in[d % SETBUFS], 16)

            def load_rest(c, g):
                base = value((c * GRP + g) * (2 * F * N) + 4 * SETS * N)
                if not first_group(c, g):
                    used = worked_out(sp, step_at(*before(c, g), 2) + 1)
                    sp.wait_ge(prod_ready, used)
                sp.dma_start(x0_rest[:].rearrange("p s n -> p (s n)"),
                             AP(tensor=x0_twice.tensor, offset=base,
                                ap=[[0, P], [1, REST * N]])).then_inc(rest_in, 16)

            def replicate(c, g):
                there = worked_out(sp, group(c, g) + 1)
                if not (isinstance(c, int) and group(c, g) < 2):
                    used = worked_out(sp, step_at(*before(*before(c, g)), 1 + STEPS) + 1)
                    sp.wait_ge(prod_ready, used)
                sp.wait_ge(x1_ready, there)
                for q in range(4):
                    rows = x1[q:P:4, :]
                    sp.dma_start(x1_rep[:, g % 2, q, :],
                                 AP(tensor=rows.tensor, offset=rows.offset,
                                    ap=[list(rows.ap[0]), [0, 4], [1, N]])).then_inc(rep_in[g % 2], 16)

            load_pairs(0, 0)
            load_rest(0, 0)
            for s in range(SETBUFS):
                load_set(0, 0, s)
            load_pairs(0, 1)
            sp.wait_ge(weights_split, 3)
            replicate(0, 0)

            def body(c):
                for g in range(GRP):
                    two_on = after(*after(c, g))
                    more = not (isinstance(two_on[0], int) and two_on[0] >= CHUNKS)
                    if more:
                        load_pairs(*two_on)
                    if not is_last(c, g):
                        load_rest(*after(c, g))
                        replicate(*after(c, g))
                    for s in range(SETBUFS, SETS):
                        load_set(c, g, s)
                    if not is_last(c, g):
                        for s in range(SETBUFS):
                            load_set(*after(c, g), s)

            chunks(sp, body, None)
            sp.wait_ge(out_stored, 16 * CHUNKS)

        @block.gpsimd
        def _(pool):
            pool.memset(ident[:], 0.0).then_inc(ident_ready, 1)
            pool.wait_ge(ident_ready, 1)
            pool.affine_select(out=ident[:], in_=ident[:], compare_op=ALU.not_equal, fill=1.0, base=0,
                               pattern=[[-1, P]], channel_multiplier=1).then_inc(ident_ready, 1)
            pool.wait_ge(ids_in, 16)
            for c in range(CHUNKS):
                if c:
                    pool.wait_ge(tr_ready, tr_x0T(c - 1, GRP - 1) + 1)
                for f in range(F):
                    pool.indirect_dma_start(emb[:, f, :], None, tables[f],
                                            bass.IndirectOffsetOnAxis(ap=ids_sb[:, c, f:f + 1], axis=0)
                                            ).then_inc(gathered, 16)

        @block.vector
        def _(dve):
            dve.memset(x0R[:, :, F:FB], 1.0).then_inc(ones_set, 1)
            dve.wait_ge(ident_ready, 2)
            dve.reduce_sum(own_sample[:], ident[:].rearrange("p (d j) -> p j d", j=J), AX.X).then_inc(setup_done, 1)
            dve.reduce_sum(own_shift[:], ident[0:R1, 0:R1].rearrange("p (f k) -> p k f", k=KK),
                           AX.X).then_inc(setup_done, 1)
            dve.wait_ge(setup_done, 2)
            dve.tensor_scalar(keep[:], own_shift[:], -1.0, 1.0, ALU.mult, ALU.add).then_inc(setup_done, 1)
            dve.wait_ge(filter1_in, 32)
            dve.wait_ge(setup_done, 3)
            dve.tensor_scalar(f0T_sb[:, 0, :], f0T_sb[:, 0, :], keep[:, 0:1], None, ALU.mult).then_inc(setup_done, 1)
            dve.wait_ge(setup_done, 4)
            dve.tensor_tensor(f0_sb, f0_sb, f0T_sb, ALU.add).then_inc(setup_done, 1)
            dve.wait_ge(setup_done, 5)
            dve.tensor_scalar(f0_sb[:, T1 - 1, :], f0_sb[:, T1 - 1, :], keep[:, KK - 1:KK], None,
                              ALU.mult).then_inc(setup_done, 1)
            dve.wait_ge(setup_done, 6)
            dve.tensor_copy(w1_native[:, 0:2, :], f0_sb[:, 2:4, :]).then_inc(setup_done, 1)
            dve.tensor_copy(w1_native[:, 2:3, :], f0_sb[:, 6:7, :]).then_inc(setup_done, 1)
            f0_split = prod_flat[0:R1, 0:2 * 4 * M].rearrange("p (h c m) -> p h c m", h=2, m=M)[:, :, 0:SPLIT, :]
            for n, (low, whole, high) in enumerate((
                    (w1_low[:].rearrange("p (h c) m -> p h c m", h=2), f0_split,
                     w1_high[:].rearrange("p (h c) m -> p h c m", h=2)),
                    (w2_low[:], f1_split, w2_high[:]),
                    (w2_rest_low[:], f1_rest, w2_rest_high[:]))):
                dve.wait_ge(weights_high, n + 1)
                dve.tensor_tensor(low, whole, high.bitcast(fp32), ALU.subtract).then_inc(weights_split, 1)
            dve.wait_ge(setup_done, 8)
            dve.wait_ge(weights_split, 3)

            def product(n, rows, tiles, operands):
                wait(dve, native_used, n - (NRING - 1))
                wait(dve, low_ready, n - (SRING - 1))
                split_at = SPLIT * place(n, SRING)
                native_at = SPLIT * SRING + (4 - SPLIT) * place(n, NRING)
                if tiles == 2 * SPLIT:
                    whole = prod[0:rows, split_at, :]
                    out_ap = AP(tensor=whole.tensor, offset=whole.offset,
                                ap=[list(whole.ap[0]), [(native_at - split_at) * N, 2], [N, SPLIT], [1, N]])
                    a, b = operands(0, tiles)
                    dve.tensor_tensor(out_ap, a.rearrange("p (h c) n -> p h c n", h=2),
                                      b.rearrange("p (h c) n -> p h c n", h=2), ALU.mult).then_inc(prod_ready, 1)
                else:
                    dve.tensor_tensor(prod[0:rows, split_at:split_at + SPLIT, :], *operands(0, SPLIT), ALU.mult)
                    dve.tensor_tensor(prod[0:rows, native_at:native_at + tiles - SPLIT, :],
                                      *operands(SPLIT, tiles), ALU.mult).then_inc(prod_ready, 1)

            def low(n, rows):
                dve.wait_ge(high_ready, value(n + 1))
                wait(dve, split_used, n - 1)
                split_at = SPLIT * place(n, SRING)
                dve.tensor_tensor(prod_low[0:rows, place(n, 2), :, :], prod[0:rows, split_at:split_at + SPLIT, :],
                                  prod_high[0:rows, place(n, 2), :, :].bitcast(fp32),
                                  ALU.subtract).then_inc(low_ready, 1)

            def repeated(ap, rows, times):
                return ap.unsqueeze(1).broadcast_to([rows, times, N])

            def layer1(c, g, half):
                lo, hi = STEP1[half]
                if half == 0:
                    dve.wait_ge(pairs_in, value(32 * (group(c, g) + 1)))
                product(layer1_step(c, g, half), R1, hi - lo,
                        lambda a, b: (pair_b[:, lo + a:lo + b, :], repeated(pair_a[:], R1, b - a)))

            def rest(c, g):
                dve.wait_ge(rest_in, value(16 * (group(c, g) + 1)))
                dve.wait_ge(x1_ready, value(group(c, g) + 1))
                product(step_at(c, g, 2), P, REST,
                        lambda a, b: (x0_rest[:, a:b, :], repeated(x1[:], P, b - a)))

            def one_set(c, g, s):
                d = SETS * g + s
                if s == 0:
                    dve.wait_ge(rep_in[g % 2], value(64 * (2 * c + g // 2 + 1)))
                dve.wait_ge(sets_in[d % SETBUFS], value(16 * ((SETS * GRP // SETBUFS) * c + d // SETBUFS + 1)))
                product(step_at(c, g, 3 + s), P, 4,
                        lambda a, b: (x1_rep[:, g % 2, a:b, :], repeated(x0_set[:, d % SETBUFS, :], P, b - a)))

            def part(c, g):
                dve.wait_ge(x1_ready, value(group(c, g) + 1))
                dve.reduce_sum(r1_part[:, UG * g:UG * (g + 1), :],
                               x1[:].rearrange("p (u d j) -> p u j d", d=D, j=J),
                               AX.X).then_inc(parts_ready, 1)

            layer1(0, 0, 0)
            layer1(0, 0, 1)
            low(0, R1)
            low(1, R1)

            def body(c):
                for g in range(GRP):
                    start = isinstance(c, int) and c == 0 and g == 0
                    for j in range(2 if is_last(c, g) else 0, PER):
                        if j < 2:
                            layer1(*after(c, g), j)
                        elif j == 2:
                            rest(c, g)
                        else:
                            one_set(c, g, j - 3)
                        if not (start and j == 0):
                            of_layer1 = 1 <= j <= 2 and not is_last(c, g)
                            low(step_at(c, g, j) - 1, R1 if of_layer1 else P)
                        if start and j == 1:
                            part(c, g)
                    if g == GRP - 1:
                        dve.wait_ge(parts_ready, value(GRP * (c + 1)))
                        if not (isinstance(c, int) and c == 0):
                            dve.wait_ge(top_summed, value(top_use(c - 1, 1) + 1))
                        dve.tensor_copy(r1[:], r1_part[:].rearrange("p u j -> p (u j)")).then_inc(r1_ready, 1)
                        dve.wait_ge(r1_ready, value(c + 1))
                    if not is_last(c, g):
                        part(*after(c, g))

            def end():
                low(step_at(LASTC, GRP - 1, PER - 1), P)

            chunks(dve, body, end)

        @block.scalar
        def _(act):
            def evac(dst, idx, src):
                act.wait_ge(tr_ready, value(idx + 1))
                act.activation(dst, src, ACT.Copy).then_inc(tr_evac, 1)

            def x0T_batch(c, k):
                if k == 0 and not (isinstance(c, int) and c == 0):
                    for g in range(GRP):
                        act.wait_ge(x0_stored[g], value(32 * c))
                evac(x0T[:].rearrange("f (u d j) -> f d u j", d=D, j=J)[:, DB * k:DB * (k + 1)], tr_x0T(c, k),
                     p_tr[place(tr_x0T(c, k), 2)][0:F, :].rearrange("f (d u j) -> f d u j", u=U, j=J))

            def x0_store(c, g):
                act.wait_ge(tr_evac, value(tr_x0T(c, GRP - 1) + 1))
                cols = slice(g * N, (g + 1) * N)
                base = (c * GRP + g) * (2 * F * N)
                act.dma_start(AP(tensor=x0_twice.tensor, offset=value(base), ap=[[N, F], [F * N, 2], [1, N]]),
                              x0T[:, cols].unsqueeze(1).broadcast_to([F, 2, N])).then_inc(x0_stored[g], 16)
                act.dma_start(AP(tensor=x0_by_set.tensor, offset=value((c * GRP + g) * (4 * SETS * N)),
                                 ap=[[N, SETS], [SETS * N, 4], [1, N]]),
                              x0T[0:4 * SETS, cols]).then_inc(x0_stored[g], 16)

            def x0R_batch(c, k):
                if not (isinstance(c, int) and c == 0):
                    act.wait_ge(diag_ready, value(J * GRP * c))
                evac(x0R[:, 8 * k:8 * k + 8, 0:F], tr_x0R(c, k),
                     p_tr[place(tr_x0R(c, k), 2)][:, 0:8 * FB].rearrange("p (u f) -> p u f", f=FB)[:, :, 0:F])

            def high(n, rows):
                act.wait_ge(prod_ready, value(n + 1))
                wait(act, split_used, n - 1)
                split_at = SPLIT * place(n, SRING)
                act.activation(prod_high[0:rows, place(n, 2), :, :], prod[0:rows, split_at:split_at + SPLIT, :],
                               ACT.Copy).then_inc(high_ready, 1)

            def x1_out(c, g):
                act.wait_ge(split_used, value(layer1_step(c, g, 1) + 1))
                if not (isinstance(c, int) and group(c, g) == 0):
                    pc, pg = before(c, g)
                    act.wait_ge(parts_ready, value(group(pc, pg) + 1))
                    act.wait_ge(rep_in[pg % 2], value(64 * (2 * pc + pg // 2 + 1)))
                    act.wait_ge(prod_ready, value(step_at(pc, pg, 2) + 1))
                act.activation(x1[:], p_x1[:], ACT.Copy).then_inc(x1_ready, 1)

            def x2_out(c, g):
                act.wait_ge(split_used, value(step_at(c, g, PER - 1) + 1))
                act.activation(x2[:].rearrange("p u n -> p (u n)"), p_x2[g % 2][:], ACT.Copy).then_inc(x2_ready, 1)

            def x2T_out(c, g):
                idx = tr_x2T(c, g)
                evac(x2T[:].rearrange("p u m -> p (u m)"), idx, p_tr[place(idx, 2)][:])

            def diag(c, g, half):
                if g == 0 and half == 0:
                    act.wait_ge(tr_evac, value(tr_x0R(c, 1) + 1))
                for j in range(J // 2 * half, J // 2 * (half + 1)):
                    act.activation(x0_diag[:, :, j, :], x0R[:, UG * g:UG * (g + 1), :], ACT.Copy,
                                   scale=own_sample[:, j:j + 1]).then_inc(diag_ready, 1)

            def cross_out(c, g, units):
                for u in units:
                    act.wait_ge(cross_summed, value(UG * group(c, g) + u + 1))
                    at = J * (UG * g + u)
                    act.activation(cross[:, at:at + J, :].rearrange("p b f -> p (b f)"),
                                   p_cross[u % 2][:, 0:J * FB], ACT.Copy).then_inc(cross_ready, 1)

            def r3_out(c):
                act.wait_ge(top_summed, value(top_use(c, 0) + 1))
                act.activation(r3[:], p_top[:, 0:P], ACT.Copy).then_inc(top_evac, 1)

            def h1_out(c):
                act.wait_ge(top_summed, value(top_use(c, 1) + 1))
                for m in range(M1):
                    last = act.activation(h1[:, m, :], p_top[:, m * P:(m + 1) * P], ACT.Relu, bias=bt1[:, m:m + 1])
                last.then_inc(top_evac, 1)

            def h2_out(c):
                act.wait_ge(top_summed, value(top_use(c, 2) + 1))
                for m in range(M2):
                    last = act.activation(h2[:, m, :], p_top[:, m * P:(m + 1) * P], ACT.Relu, bias=bt2[:, m:m + 1])
                last.then_inc(top_evac, 1)

            def y_out(c):
                act.wait_ge(top_summed, value(top_use(c, 3) + 1))
                act.activation(y_sb[:], p_top[0:1, 0:P], ACT.Copy).then_inc(top_evac, 1)
                act.wait_ge(top_evac, value(top_use(c, 3) + 1))
                act.dma_start(AP(tensor=out.tensor, offset=value(c * P), ap=[[P, 1], [1, P]]), y_sb[:]).then_inc(out_stored, 16)

            def evacuate(c, t):
                first = isinstance(c, int) and c == 0
                final = isinstance(c, int) and c == LASTC
                g, j = t // PER, t % PER
                if j == 1 and not is_last(c, g):
                    x1_out(*after(c, g))
                if j == PER - 1:
                    x2_out(c, g)
                for k in range(GRP):
                    if k or not first:
                        if t == X2T_AT[k]:
                            x2T_out(*before(c, k))
                        if t in CONTRACT_AT[k]:
                            cross_out(*before(c, k), (CONTRACT_AT[k].index(t),))
                    if t in DIAG_AT[k]:
                        diag(c, k, DIAG_AT[k].index(t))
                if not first:
                    if t == L3_AT[-1]:
                        r3_out(c - 1)
                    if t == TOP1_AT[-1]:
                        act.wait_ge(top_in, 96)
                        h1_out(c - 1)
                    if t == TOP2_AT[-1]:
                        h2_out(c - 1)
                    if t == TOP3_AT:
                        y_out(c - 1)
                if not final:
                    if t in X0T_AT:
                        x0T_batch(c + 1, X0T_AT.index(t))
                    if X0T_AT[-1] <= t < X0T_AT[-1] + GRP:
                        x0_store(c + 1, t - X0T_AT[-1])
                    if t in X0R_AT:
                        x0R_batch(c + 1, X0R_AT.index(t))

            for k in range(2):
                act.wait_ge(top_summed, k + 1)
                act.activation(dense_T[:, k * N:(k + 1) * N], p_top[0:DC, :], ACT.Copy).then_inc(top_evac, 1)
            act.wait_ge(setup_done, 6)
            f0_split = prod_flat[0:R1, 0:2 * 4 * M].rearrange("p (h c m) -> p h c m", h=2, m=M)[:, :, 0:SPLIT, :]
            act.activation(w1_high[:].rearrange("p (h c) m -> p h c m", h=2), f0_split,
                           ACT.Copy).then_inc(weights_high, 1)
            act.wait_ge(filter2_in, 16 * (2 * SETS + 2))
            act.activation(w2_high[:], f1_split, ACT.Copy).then_inc(weights_high, 1)
            act.activation(w2_rest_high[:], f1_rest, ACT.Copy).then_inc(weights_high, 1)
            for k in range(GRP):
                x0T_batch(0, k)
            for g in range(GRP):
                x0_store(0, g)
            act.wait_ge(ones_set, 1)
            for k in range(2):
                x0R_batch(0, k)
            high(0, R1)
            high(1, R1)

            def body(c):
                for g in range(GRP):
                    for j in range(2 if is_last(c, g) else 0, PER):
                        high(step_at(c, g, j), R1 if j < 2 else P)
                        t = PER * g + j
                        if isinstance(c, int) and c == 0 and t == 0:
                            x1_out(0, 0)
                        elif isinstance(c, int) and c == 0 and t < LAG:
                            pass
                        elif t < LAG:
                            evacuate(c - 1, PER * GRP + t - LAG)
                        elif is_last(c, g) and j < 2 + LAG:
                            evacuate(c, t - LAG - 2)
                        else:
                            if is_last(c, g) and j == 2 + LAG:
                                for missing in range(PER * g, PER * g + 2):
                                    evacuate(c, missing)
                            evacuate(c, t - LAG)
                if not (isinstance(c, int) and c == 0):
                    act.wait_ge(out_stored, value(16 * c))

            def end():
                for t in range(PER * GRP - LAG, PER * GRP):
                    evacuate(LASTC, t)
                x2T_out(LASTC, GRP - 1)
                cross_out(LASTC, GRP - 1, range(UG))
                r3_out(LASTC)
                h1_out(LASTC)
                h2_out(LASTC)
                y_out(LASTC)

            chunks(act, body, end)

        @block.tensor
        def _(pe):
            def bank_free(idx):
                wait(pe, tr_evac, idx - 1)

            def x0T_waits(c, k):
                if k == 0:
                    pe.wait_ge(gathered, value(16 * F * (c + 1)))
                bank_free(tr_x0T(c, k))

            def x0T_batch(c, k):
                for i in range(DB):
                    last = pe.transpose(p_tr[place(tr_x0T(c, k), 2)][0:F, i * P:(i + 1) * P], emb[:, :, DB * k + i], ident[:])
                last.then_inc(tr_ready, 1)

            def x0R_waits(c, k):
                pe.wait_ge(tr_evac, value(tr_x0T(c, GRP - 1) + 1))
                bank_free(tr_x0R(c, k))

            def x0R_batch(c, k):
                for i in range(8):
                    u = 8 * k + i
                    last = pe.transpose(p_tr[place(tr_x0R(c, k), 2)][:, i * FB:i * FB + F], x0T[:, u * P:(u + 1) * P],
                                        ident[0:F, 0:F])
                last.then_inc(tr_ready, 1)

            def x2T_batch(c, g):
                pe.wait_ge(x2_ready, value(group(c, g) + 1))
                idx = tr_x2T(c, g)
                bank_free(idx)
                for i in range(UG):
                    last = pe.transpose(p_tr[place(idx, 2)][:, i * P:(i + 1) * P], x2[:, i, :], ident[:])
                last.then_inc(tr_ready, 1)

            def contract(c, g, units):
                for u in units:
                    if u == 0:
                        pe.wait_ge(tr_evac, value(tr_x2T(c, g) + 1))
                        pe.wait_ge(diag_ready, value(J * (group(c, g) + 1)))
                    wait(pe, cross_ready, UG * group(c, g) + u - 1)
                    pe.matmul(p_cross[u % 2][:, 0:J * FB], x2T[:, u, :],
                              x0_diag[:, u, :, :].rearrange("p j f -> p (j f)"),
                              start=True, stop=True).then_inc(cross_summed, 1)

            def layer3(c, fields):
                for f in fields:
                    if f == 0:
                        pe.wait_ge(cross_ready, value(U * (c + 1)))
                        pe.wait_ge(filter3_in, 16)
                        pe.wait_ge(top_evac, value(top_use(c, 0)))
                    last = pe.matmul(p_top[:, 0:P], w3[:, f, :], cross[:, :, f], start=(f == 0), stop=(f == F - 1))
                    if f == F - 1:
                        last.then_inc(top_summed, 1)

            def top1(c, part):
                if part == 0:
                    pe.wait_ge(top_evac, value(top_use(c, 1)))
                    pe.wait_ge(r1_ready, value(c + 1))
                    pe.wait_ge(top_in, 96)
                cols = slice(part * P, (part + 1) * P)
                pe.matmul(p_top[:, cols], wt1[:, 0, cols], r1[:], start=True, stop=False)
                pe.matmul(p_top[:, cols], wt1[:, 1, cols], cross[:, :, F], start=False, stop=False)
                pe.matmul(p_top[:, cols], wt1[:, 2, cols], r3[:], start=False, stop=False)
                last = pe.matmul(p_top[:, cols], wt1_dense[:, cols], dense_T[:, bass.ds(value(c * P), P)],
                                 start=False, stop=True)
                if part == M1 - 1:
                    last.then_inc(top_summed, 1)

            def top2(c, part):
                if part == 0:
                    pe.wait_ge(top_evac, value(top_use(c, 2)))
                for k in range(M1):
                    last = pe.matmul(p_top[:, part * P:(part + 1) * P], wt2[:, k, part * P:(part + 1) * P], h1[:, k, :],
                                     start=(k == 0), stop=(k == M1 - 1))
                if part == M2 - 1:
                    last.then_inc(top_summed, 1)

            def top3(c):
                pe.wait_ge(top_evac, value(top_use(c, 3)))
                for k in range(M2):
                    last = pe.matmul(p_top[0:1, 0:P], wt3[:, k:k + 1], h2[:, k, :], start=(k == 0), stop=(k == M2 - 1))
                last.then_inc(top_summed, 1)

            def ahead(c, t):
                if isinstance(c, int) and c == LASTC:
                    return
                if t in X0T_AT:
                    x0T_waits(c + 1, X0T_AT.index(t))
                if t in X0R_AT:
                    x0R_waits(c + 1, X0R_AT.index(t))

            def between(c, t):
                first = isinstance(c, int) and c == 0
                final = isinstance(c, int) and c == LASTC
                for k in range(GRP):
                    if k or not first:
                        if t == X2T_AT[k]:
                            x2T_batch(*before(c, k))
                        if t in CONTRACT_AT[k]:
                            contract(*before(c, k), (CONTRACT_AT[k].index(t),))
                if not first:
                    if t in L3_AT:
                        at = L3_FIELDS * L3_AT.index(t)
                        layer3(c - 1, range(at, min(at + L3_FIELDS, F)))
                    if t in TOP1_AT:
                        top1(c - 1, TOP1_AT.index(t))
                    if t in TOP2_AT:
                        top2(c - 1, TOP2_AT.index(t))
                    if t == TOP3_AT:
                        top3(c - 1)
                if not final:
                    if t in X0T_AT:
                        x0T_batch(c + 1, X0T_AT.index(t))
                    if t in X0R_AT:
                        x0R_batch(c + 1, X0R_AT.index(t))

            def step(n, rows, bank, natives, highs, lows, start, stop, before_last):
                pe.wait_ge(prod_ready, value(n + 1))
                native_at = SPLIT * SRING + (4 - SPLIT) * place(n, NRING)
                for i, weights in enumerate(natives):
                    last = pe.matmul(bank[:], weights, prod[0:rows, native_at + i, :],
                                     start=(start and i == 0), stop=False)
                last.then_inc(native_used, 1)
                pe.wait_ge(low_ready, value(n + 1))
                at = place(n, 2)
                passes = [(highs[i], prod_high[0:rows, at, i, :]) for i in range(SPLIT)]
                passes += [(lows[i], prod_high[0:rows, at, i, :]) for i in range(SPLIT)]
                passes += [(highs[i], prod_low[0:rows, at, i, :]) for i in range(SPLIT)]
                for i, (weights, part) in enumerate(passes):
                    final = i == len(passes) - 1
                    if final:
                        before_last()
                    last = pe.matmul(bank[:], weights, part, start=False, stop=(stop and final))
                last.then_inc(split_used, 1)

            def layer1(c, g, half, before_last):
                if half == 0:
                    wait(pe, x1_ready, group(c, g))
                lo, hi = STEP1[half]
                step(layer1_step(c, g, half), R1, p_x1,
                     [w1_native[:, 2 * half + i, :] for i in range(hi - lo - SPLIT)],
                     [w1_high[:, SPLIT * half + i, :] for i in range(SPLIT)],
                     [w1_low[:, SPLIT * half + i, :] for i in range(SPLIT)], half == 0, half == 1, before_last)

            def layer2(c, g, j, before_last):
                if j == 2:
                    wait(pe, x2_ready, group(c, g) - 1)
                    natives = [w2_rest[:, i, :] for i in range(REST - SPLIT)]
                    highs, lows = w2_rest_high, w2_rest_low
                    high, low = ([w[:, i, :] for i in range(SPLIT)] for w in (highs, lows))
                else:
                    natives = [w2_native[:, j - 3, i, :] for i in range(4 - SPLIT)]
                    high, low = ([w[:, j - 3, i, :] for i in range(SPLIT)] for w in (w2_high, w2_low))
                step(step_at(c, g, j), P, p_x2[g % 2], natives, high, low, j == 2, j == PER - 1, before_last)

            pe.wait_ge(ident_ready, 2)
            pe.wait_ge(dense_in, 16)
            for k in range(2):
                wait(pe, top_evac, k)
                for i in range(4):
                    last = pe.transpose(p_top[0:DC, i * P:(i + 1) * P], dense_sb[:, 4 * k + i, :], ident[:])
                last.then_inc(top_summed, 1)
            for k in range(GRP):
                x0T_waits(0, k)
                x0T_batch(0, k)
            for k in range(2):
                x0R_waits(0, k)
                x0R_batch(0, k)
            pe.wait_ge(setup_done, 8)
            pe.wait_ge(weights_split, 1)
            for half in range(2):
                layer1(0, 0, half, lambda: None)
            pe.wait_ge(filter2_in, 16 * (2 * SETS + 2))
            pe.wait_ge(weights_split, 3)

            def body(c):
                for g in range(GRP):
                    for j in range(2 if is_last(c, g) else 0, PER):
                        t = PER * g + j
                        if j < 2:
                            layer1(*after(c, g), j, lambda: ahead(c, t))
                        else:
                            layer2(c, g, j, lambda: ahead(c, t))
                        if is_last(c, g) and j == 2:
                            between(c, t - 2)
                            between(c, t - 1)
                        between(c, t)

            def end():
                x2T_batch(LASTC, GRP - 1)
                contract(LASTC, GRP - 1, range(UG))
                layer3(LASTC, range(F))
                for part in range(M1):
                    top1(LASTC, part)
                for part in range(M2):
                    top2(LASTC, part)
                top3(LASTC)

            chunks(pe, body, end)


def kernel(**inputs):
    import numpy as np
    import concourse.bacc as bacc
    from concourse.bass_utils import run_bass_kernel_spmd

    nc = bacc.Bacc("TRN2", target_bir_lowering=False, num_devices=1)
    arrays, handles = {}, {}
    for name, value in inputs.items():
        a = np.ascontiguousarray(value)
        arrays[f"in_{name}"] = a
        handles[name] = nc.dram_tensor(f"in_{name}", a.shape, mybir.dt.from_np(a.dtype), kind="ExternalInput").ap()
    batch, fields = inputs["ids"].shape
    out = nc.dram_tensor("out", (batch, 1), mybir.dt.float32, kind="ExternalOutput").ap()
    build_cin_tower(nc, handles["dense_ctx"], handles["ids"], [handles[f"tbl_{f}"] for f in range(fields)],
                    handles["W_top1"], handles["b_top1"], handles["W_top2"], handles["b_top2"], handles["W_top3"],
                    handles["L0_rec_f0"], handles["L0_rec_f1"], handles["L0_rec_f2"], out)
    r = run_bass_kernel_spmd(nc, [arrays], core_ids=[0])
    return r.results[0]["out"]
```

```python
import concourse.bass as bass
from concourse import mybir
from contextlib import ExitStack


class Linear:

    def __init__(self, register, times, plus):
        self.register, self.times, self.plus = register, times, plus

    def __add__(self, k):
        return Linear(self.register, self.times, self.plus + k)

    def __sub__(self, k):
        return self + -k

    def __mul__(self, k):
        return Linear(self.register, self.times * k, self.plus * k)

    __radd__, __rmul__ = __add__, __mul__


def value(x):
    return x if isinstance(x, int) else x.register * x.times + x.plus


def build_cin_tower(nc, dense_ctx, ids, tables, W_top1, b_top1, W_top2, b_top2, W_top3, f0, f1, f2, out):
    fp32 = mybir.dt.float32
    fp32r = mybir.dt.float32r
    ALU = mybir.AluOpType
    ACT = mybir.ActivationFunctionType
    AX = mybir.AxisListType
    AP = bass.AP

    B, F = ids.shape
    D = tables[0].shape[1]
    M = f0.shape[1]
    P = 128
    CHUNKS = B // P
    GRP = 4
    DB = D // GRP
    N = P // GRP * D
    KK = 3
    SHIFTS = (F + 1) // 2
    T1 = -(-SHIFTS // KK)
    R1 = F * KK
    PARTS = ((0, 1), (1, 4), (4, T1))
    BF = 4
    BLOCKS = -(-F // BF)
    BY_ACT = (0, 3, 5, 7)
    BY_DVE = tuple(b for b in range(BLOCKS) if b not in BY_ACT)
    YBANKS = 5
    J = P // D
    U = P // J
    UG = U // GRP
    FB = F + 1
    H1, H2 = W_top1.shape[1], W_top2.shape[1]
    M1, M2 = H1 // P, H2 // P
    DC = dense_ctx.shape[1]
    LASTC = CHUNKS - 1
    GB = UG * BLOCKS
    ACTS = len(BY_ACT)
    SUMS = F - BF * ACTS
    JOINS = 5
    L1_PROD, L1_HIGH, L1_LOW, L1_MULTIPLY = ([4 * t + at for t in range(T1)] for at in (0, 2, 3, 9))
    X1_HIGH, X1_LOW = 34, 35
    LAG, TR_LAG = 1, 1
    CONTRACT_AT = ((2, 8, 14, 20), (56, 62, 68, 74), (82, 88, 94, 100), (122, 128, 134, 140))
    X0R_SECOND_AT, X0T_AT, X0R_FIRST_AT = 11, (86, 92, 98, 104), 150
    L3_FIELDS = 4
    L3_AT = tuple(26 + 2 * i for i in range(-(-F // L3_FIELDS)))
    TOP1_AT, TOP2_AT, TOP3_AT = (50, 51, 53, 54), (61, 63), 70
    DIAG_AT = ((22, 25, 28, 31), (75, 76, 77, 79), (101, 102, 104, 105), (142, 144, 147, 149))
    STORE_AT = (106, 107, 109, 111)
    GATHERS_FROM = 10
    PER_UNIT = 3

    x0_twice = nc.dram_tensor("x0_twice", [CHUNKS, GRP, 2 * F, N], fp32).ap()
    f0_fg = nc.dram_tensor("f0_fg", [F, 2 * F, M], fp32).ap()
    f0_gf = nc.dram_tensor("f0_gf", [F, 2 * F, M], fp32).ap()

    with ExitStack() as ctx:
        def sb(name, shape, dt=fp32):
            return ctx.enter_context(nc.sbuf_tensor(name, shape, dt))

        def ps(name, shape):
            return ctx.enter_context(nc.psum_tensor(name, shape, fp32))

        def sem(name):
            return ctx.enter_context(nc.semaphore(name))

        w1_high = sb("w1_high", [R1, T1, M], fp32r)
        w1_low = sb("w1_low", [R1, T1, M], fp32r)
        w2_high = sb("w2_high", [P, F, M], fp32r)
        w2_low = sb("w2_low", [P, F, M], fp32r)
        w3 = sb("w3", [P, F, M])
        wt1 = sb("wt1", [P, 3, H1])
        wt1_dense = sb("wt1_dense", [DC, H1])
        wt2 = sb("wt2", [P, M1, H2])
        wt3 = sb("wt3", [P, M2])
        bt1 = sb("bt1", [P, M1])
        bt2 = sb("bt2", [P, M2])
        ident = sb("ident", [P, P])
        own_sample = sb("own_sample", [P, J])
        own_shift = sb("own_shift", [R1, KK])
        keep = sb("keep", [R1, KK])
        ids_sb = sb("ids_sb", [P, F], mybir.dt.int32)
        emb = sb("emb", [P, F, D])
        dense_T = sb("dense_T", [DC, B])
        x0T = sb("x0T", [F, D * P])
        pair_a = sb("pair_a", [R1, N])
        pair_b = sb("pair_b", [R1, T1, N])
        prod = sb("prod", [R1, 2, N])
        prod_high = sb("prod_high", [R1, 2, N], fp32r)
        prod_low = sb("prod_low", [R1, 2, N], fp32r)
        x1_high = sb("x1_high", [P, 2, N], fp32r)
        x1_low = sb("x1_low", [P, 2, N], fp32r)
        scaled_y = sb("scaled_y", [P, 2, ACTS, BF, P])
        sum_y = sb("sum_y", [P, 2, BF, P])
        r1_part = sb("r1_part", [P, U, J])
        r1 = sb("r1", [P, P])
        x2T = sb("x2T", [P, 2, UG, P])
        x0R = sb("x0R", [P, U, FB])
        x0_diag = sb("x0_diag", [P, UG, J, FB])
        cross = sb("cross", [P, P, FB])
        r3 = sb("r3", [P, P])
        h1 = sb("h1", [P, M1, P])
        h2 = sb("h2", [P, M2, P])
        y_sb = sb("y_sb", [1, P])
        scaled_flat = scaled_y[:].rearrange("p a b c n -> p (a b c n)")
        f0_sb = scaled_flat[0:R1, 0:T1 * M].rearrange("p (c m) -> p c m", m=M)
        f0T_sb = scaled_flat[0:R1, T1 * M:2 * T1 * M].rearrange("p (c m) -> p c m", m=M)
        f1_sb = cross[:].rearrange("p b f -> p (b f)")[:, 0:F * M].rearrange("p (f m) -> p f m", m=M)
        dense_sb = x2T[:, 0, 0, :].rearrange("p (c k) -> p c k", k=DC)

        p_x1 = ps("p_x1", [P, N])
        p_y = [ps(f"p_y_{i}", [P, BF * P]) for i in range(YBANKS)]
        p_cross = ps("p_cross", [P, N])
        p_top = ps("p_top", [P, N])

        filter1_copied = sem("filter1_copied")
        filter1_in = sem("filter1_in")
        filter2_in = sem("filter2_in")
        filter3_in = sem("filter3_in")
        top_in = sem("top_in")
        dense_in = sem("dense_in")
        ids_in = sem("ids_in")
        gathered = sem("gathered")
        ident_ready = sem("ident_ready")
        setup_done = sem("setup_done")
        ones_set = sem("ones_set")
        x0_stored = [sem(f"x0_stored_{g}") for g in range(GRP)]
        pair_a_in = sem("pair_a_in")
        pair_b_in = [sem(f"pair_b_in_{i}") for i in range(len(PARTS))]
        weights_high = sem("weights_high")
        weights_split = sem("weights_split")
        prod_ready = sem("prod_ready")
        high_ready = sem("high_ready")
        low_ready = sem("low_ready")
        prod_used = sem("prod_used")
        x1_high_ready = sem("x1_high_ready")
        x1_low_ready = sem("x1_low_ready")
        y_ready = sem("y_ready")
        scaled = sem("scaled")
        summed = sem("summed")
        joined = sem("joined")
        parts_ready = sem("parts_ready")
        r1_ready = sem("r1_ready")
        tr_ready = sem("tr_ready")
        tr_evac = sem("tr_evac")
        diag_ready = sem("diag_ready")
        cross_summed = sem("cross_summed")
        cross_ready = sem("cross_ready")
        top_summed = sem("top_summed")
        top_evac = sem("top_evac")
        out_stored = sem("out_stored")

        def is_last(c, g):
            return isinstance(c, int) and c == LASTC and g == GRP - 1

        def group(c, g):
            return GRP * c + g

        def unit(c, g, u):
            return U * c + UG * g + u

        def after(c, g):
            return (c, g + 1) if g + 1 < GRP else (c + 1, 0)

        def before(c, g):
            return (c, g - 1) if g else (c - 1, GRP - 1)

        def place(x, ring):
            if isinstance(x, int):
                return x % ring
            assert x.times % ring == 0
            return x.plus % ring

        def x0T_bank(c, k):
            return p_y[k] if isinstance(c, int) and c == 0 else p_top

        def tr_x0T(c, k):
            return 6 * c + k

        def tr_x0R(c, k):
            return 6 * c + GRP + k

        def top_use(c, k):
            return 2 + 4 * c + k

        def wait(eng, semaphore, count):
            if not (isinstance(count, int) and count <= 0):
                eng.wait_ge(semaphore, value(count))

        def worked_out(eng, count):
            return count if isinstance(count, int) else eng.snap(eng.to_reg(value(count)))

        def chunks(eng, body, end):
            body(0)
            with eng.Fori(0, LASTC - 2) as before_c:
                body(Linear(before_c, 1, 1))
            body(LASTC - 1)
            body(LASTC)
            if end:
                end()

        def has_second_next(c):
            return isinstance(c, Linear) or c + 2 < CHUNKS

        block = ctx.enter_context(nc.Block())

        @block.sync
        def _(sp):
            sp.dma_start(ids_sb[:], ids[0:P, :]).then_inc(ids_in, 16)
            sp.dma_start(f0_fg[:, 0:F, :], f0.rearrange("(f g) m -> f g m", g=F)).then_inc(filter1_copied, 16)
            sp.dma_start(f0_fg[:, F:2 * F, :], f0.rearrange("(f g) m -> f g m", g=F)).then_inc(filter1_copied, 16)
            sp.dma_start(f0_gf[:, 0:F, :], f0.rearrange("(f g) m -> g f m", g=F)).then_inc(filter1_copied, 16)
            sp.dma_start(f0_gf[:, F:2 * F, :], f0.rearrange("(f g) m -> g f m", g=F)).then_inc(filter1_copied, 16)
            sp.dma_start(dense_sb, dense_ctx.rearrange("(c p) k -> p c k", p=P)).then_inc(dense_in, 16)
            sp.dma_start(f1_sb, f1.rearrange("(f g) m -> g f m", g=P)).then_inc(filter2_in, 16)
            sp.wait_ge(filter1_copied, 64)
            for dst, src in ((f0_sb, f0_fg), (f0T_sb, f0_gf)):
                sp.dma_start(dst, AP(tensor=src.tensor, offset=0,
                                     ap=[[(2 * F + 1) * M, F], [T1 * M, KK], [1, T1 * M]])).then_inc(filter1_in, 16)
            sp.dma_start(w3[:], AP(tensor=f2.tensor, offset=0,
                                   ap=[[M, P], [M * M, F], [1, M]])).then_inc(filter3_in, 16)
            sp.dma_start(wt1[:], W_top1[0:3 * P, :].rearrange("(k p) n -> p k n", p=P)).then_inc(top_in, 16)
            sp.dma_start(wt1_dense[:], W_top1[3 * P:3 * P + DC, :]).then_inc(top_in, 16)
            sp.dma_start(wt2[:], W_top2.rearrange("(k p) n -> p k n", p=P)).then_inc(top_in, 16)
            sp.dma_start(wt3[:], W_top3.rearrange("(k p) n -> p (k n)", p=P),
                         allow_slow_non_contiguous=True).then_inc(top_in, 16)
            sp.dma_start(bt1[:], b_top1.rearrange("(k p) -> p k", p=P),
                         allow_slow_non_contiguous=True).then_inc(top_in, 16)
            sp.dma_start(bt2[:], b_top2.rearrange("(k p) -> p k", p=P),
                         allow_slow_non_contiguous=True).then_inc(top_in, 16)

            def load_ids(c):
                sp.wait_ge(gathered, value(16 * F * c))
                sp.dma_start(ids_sb[:], AP(tensor=ids.tensor, offset=value(P * F * c),
                                           ap=[[F, P], [1, F]])).then_inc(ids_in, 16)

            def first_group(c, g):
                return isinstance(c, int) and c == 0 and g == 0

            def load_pair_b(c, g, part):
                lo, hi = PARTS[part]
                base = value((c * GRP + g) * (2 * F * N) + lo * N)
                stored = worked_out(sp, 16 * (c + 1))
                used = 0 if first_group(c, g) else worked_out(sp, T1 * group(*before(c, g)) + hi)
                sp.wait_ge(x0_stored[g], stored)
                if not first_group(c, g):
                    sp.wait_ge(prod_ready, used)
                sp.dma_start(pair_b[:, lo:hi, :].rearrange("p c n -> p (c n)"),
                             AP(tensor=x0_twice.tensor, offset=base,
                                ap=[[N, F], [T1 * N, KK], [1, (hi - lo) * N]])).then_inc(pair_b_in[part], 16)

            def load_pair_a(c, g):
                base = value((c * GRP + g) * (2 * F * N))
                stored = worked_out(sp, 16 * (c + 1))
                used = 0 if first_group(c, g) else worked_out(sp, T1 * group(c, g))
                sp.wait_ge(x0_stored[g], stored)
                if not first_group(c, g):
                    sp.wait_ge(prod_ready, used)
                sp.dma_start(pair_a[:], AP(tensor=x0_twice.tensor, offset=base,
                                           ap=[[N, F], [0, KK], [1, N]])).then_inc(pair_a_in, 16)

            def load_pairs(c, g):
                for part in range(len(PARTS) - 1):
                    load_pair_b(c, g, part)
                load_pair_a(c, g)
                load_pair_b(c, g, len(PARTS) - 1)

            load_ids(1)
            load_pair_a(0, 0)
            for part in range(len(PARTS)):
                load_pair_b(0, 0, part)
            load_pairs(0, 1)

            def body(c):
                for g in range(GRP):
                    if g == GRP - 1 and has_second_next(c):
                        load_ids(c + 2)
                    two_on = after(*after(c, g))
                    if not (isinstance(two_on[0], int) and two_on[0] >= CHUNKS):
                        load_pairs(*two_on)

            chunks(sp, body, None)
            sp.wait_ge(out_stored, 16 * CHUNKS)

        @block.gpsimd
        def _(pool):
            pool.memset(ident[:], 0.0).then_inc(ident_ready, 1)
            pool.wait_ge(ident_ready, 1)
            pool.affine_select(out=ident[:], in_=ident[:], compare_op=ALU.not_equal, fill=1.0, base=0,
                               pattern=[[-1, P]], channel_multiplier=1).then_inc(ident_ready, 1)

            def gather_waits(c):
                pool.wait_ge(ids_in, value(16 * (c + 1)))
                if not (isinstance(c, int) and c == 0):
                    pool.wait_ge(tr_ready, value(tr_x0T(c - 1, GRP - 1) + 1))

            def gather(fields):
                for f in fields:
                    pool.indirect_dma_start(emb[:, f, :], None, tables[f],
                                            bass.IndirectOffsetOnAxis(ap=ids_sb[:, f:f + 1], axis=0)
                                            ).then_inc(gathered, 16)

            def join(c, g, u):
                n = unit(c, g, u)
                blocks = scaled_y[:, u % 2]
                pool.wait_ge(scaled, value(ACTS * n + 3))
                pool.tensor_tensor(blocks[:, 1], blocks[:, 1], blocks[:, 2], ALU.add).then_inc(joined, 1)
                pool.wait_ge(scaled, value(ACTS * n + 4))
                pool.wait_ge(joined, value(JOINS * n + 1))
                pool.tensor_tensor(blocks[:, 1], blocks[:, 1], blocks[:, 3], ALU.add).then_inc(joined, 1)
                pool.wait_ge(summed, value(SUMS * (n + 1)))
                pool.wait_ge(joined, value(JOINS * n + 2))
                pool.tensor_tensor(blocks[:, 1], blocks[:, 1], sum_y[:, u % 2], ALU.add).then_inc(joined, 1)
                pool.wait_ge(joined, value(JOINS * n + 3))
                pool.tensor_tensor(blocks[:, 1, 0:2], blocks[:, 1, 0:2], blocks[:, 1, 2:4], ALU.add).then_inc(joined, 1)
                if UG * g + u == GATHERS_FROM and has_second_next(c):
                    gather_waits(c + 2)
                pool.wait_ge(joined, value(JOINS * n + 4))
                wait(pool, cross_summed, UG * (group(c, g) - 1))
                pool.tensor_tensor(x2T[:, g % 2, u, :], blocks[:, 1, 0, :], blocks[:, 1, 1, :],
                                   ALU.add).then_inc(joined, 1)

            gather_waits(0)
            gather(range(F))
            gather_waits(1)
            gather(range(PER_UNIT * (U - GATHERS_FROM)))

            def body(c):
                for i in range(U):
                    join(c, i // UG, i % UG)
                    if i >= GATHERS_FROM:
                        done, there = PER_UNIT * (i - GATHERS_FROM), has_second_next(c)
                    else:
                        done = PER_UNIT * (U - GATHERS_FROM + i)
                        there = not isinstance(c, int) or c < LASTC
                    if there:
                        gather(range(min(done, F), min(done + PER_UNIT, F)))

            chunks(pool, body, None)

        @block.vector
        def _(dve):
            dve.memset(x0R[:, :, F:FB], 1.0).then_inc(ones_set, 1)
            dve.wait_ge(ident_ready, 2)
            dve.reduce_sum(own_sample[:], ident[:].rearrange("p (d j) -> p j d", j=J), AX.X).then_inc(setup_done, 1)
            dve.reduce_sum(own_shift[:], ident[0:R1, 0:R1].rearrange("p (f k) -> p k f", k=KK),
                           AX.X).then_inc(setup_done, 1)
            dve.wait_ge(setup_done, 2)
            dve.tensor_scalar(keep[:], own_shift[:], -1.0, 1.0, ALU.mult, ALU.add).then_inc(setup_done, 1)
            dve.wait_ge(filter1_in, 32)
            dve.wait_ge(setup_done, 3)
            dve.tensor_scalar(f0T_sb[:, 0, :], f0T_sb[:, 0, :], keep[:, 0:1], None, ALU.mult).then_inc(setup_done, 1)
            dve.wait_ge(setup_done, 4)
            dve.tensor_tensor(f0_sb, f0_sb, f0T_sb, ALU.add).then_inc(setup_done, 1)
            dve.wait_ge(setup_done, 5)
            dve.tensor_scalar(f0_sb[:, T1 - 1, :], f0_sb[:, T1 - 1, :], keep[:, KK - 1:KK], None,
                              ALU.mult).then_inc(setup_done, 1)
            dve.wait_ge(setup_done, 6)
            for n, (low, whole, high) in enumerate(((w1_low, f0_sb, w1_high), (w2_low, f1_sb, w2_high))):
                dve.wait_ge(weights_high, n + 1)
                dve.tensor_tensor(low[:], whole, high[:].bitcast(fp32), ALU.subtract).then_inc(weights_split, 1)

            def form(c, g, t):
                n = T1 * group(c, g) + t
                if t == 0:
                    dve.wait_ge(pair_a_in, value(16 * (group(c, g) + 1)))
                for part in range(len(PARTS)):
                    if t == PARTS[part][0]:
                        dve.wait_ge(pair_b_in[part], value(16 * (group(c, g) + 1)))
                wait(dve, low_ready, n - 1)
                dve.tensor_tensor(prod[:, place(n, 2), :], pair_b[:, t, :], pair_a[:], ALU.mult).then_inc(prod_ready, 1)

            def low(c, g, t):
                n = T1 * group(c, g) + t
                dve.wait_ge(high_ready, value(n + 1))
                wait(dve, prod_used, n - 1)
                dve.tensor_tensor(prod_low[:, place(n, 2), :], prod[:, place(n, 2), :],
                                  prod_high[:, place(n, 2), :].bitcast(fp32), ALU.subtract).then_inc(low_ready, 1)

            def x1_in(c, g):
                dve.wait_ge(x1_high_ready, value(group(c, g) + 1))
                dve.tensor_tensor(x1_low[:, g % 2, :], p_x1[:], x1_high[:, g % 2, :].bitcast(fp32),
                                  ALU.subtract).then_inc(x1_low_ready, 1)
                dve.reduce_sum(r1_part[:, UG * g:UG * (g + 1), :],
                               p_x1[:].rearrange("p (u d j) -> p u j d", d=D, j=J), AX.X).then_inc(parts_ready, 1)

            def r1_out(c):
                dve.wait_ge(parts_ready, value(GRP * (c + 1)))
                if not (isinstance(c, int) and c == 0):
                    dve.wait_ge(top_summed, value(top_use(c - 1, 1) + 1))
                dve.tensor_copy(r1[:], r1_part[:].rearrange("p u j -> p (u j)")).then_inc(r1_ready, 1)
                dve.wait_ge(r1_ready, value(c + 1))

            def sum_block(c, g, u, b):
                n = unit(c, g, u)
                k = BLOCKS * u + b
                first = b == BY_DVE[0]
                dve.wait_ge(y_ready, value(GB * group(c, g) + k + 1))
                if first:
                    dve.wait_ge(scaled, value(ACTS * n + 1))
                    wait(dve, joined, JOINS * (n - 1))
                    if g % 2 == 0 and u == 0:
                        dve.wait_ge(tr_evac, value(tr_x0R(c, g // 2) + 1))
                for f in range(BF * b, min(BF * (b + 1), F)):
                    i = f % BF
                    at = BF * BY_DVE.index(b) + i
                    if not first:
                        dve.wait_ge(summed, value(SUMS * n + at - BF + 1))
                    dve.scalar_tensor_tensor(sum_y[:, u % 2, i, :], p_y[k % YBANKS][:, i * P:(i + 1) * P],
                                             x0R[:, UG * g + u, f:f + 1],
                                             scaled_y[:, u % 2, 0, i, :] if first else sum_y[:, u % 2, i, :],
                                             ALU.mult, ALU.add).then_inc(summed, 1)

            for t in range(T1):
                form(0, 0, t)
                if t:
                    low(0, 0, t - 1)
            low(0, 0, T1 - 1)
            x1_in(0, 0)

            def body(c):
                for g in range(GRP):
                    for k in range(GB):
                        if k % BLOCKS in BY_DVE:
                            sum_block(c, g, k // BLOCKS, k % BLOCKS)
                        if g == GRP - 1 and k == X1_LOW - 1:
                            r1_out(c)
                        if not is_last(c, g):
                            if k in L1_PROD:
                                form(*after(c, g), L1_PROD.index(k))
                            if k in L1_LOW:
                                low(*after(c, g), L1_LOW.index(k))
                            if k == X1_LOW:
                                x1_in(*after(c, g))

            chunks(dve, body, None)

        @block.scalar
        def _(act):
            def evac(dst, idx, src):
                act.wait_ge(tr_ready, value(idx + 1))
                act.activation(dst, src, ACT.Copy).then_inc(tr_evac, 1)

            def x0T_batch(c, k):
                if k == 0 and not (isinstance(c, int) and c == 0):
                    for g in range(GRP):
                        act.wait_ge(x0_stored[g], value(16 * c))
                evac(x0T[:].rearrange("f (u d j) -> f d u j", d=D, j=J)[:, DB * k:DB * (k + 1)], tr_x0T(c, k),
                     x0T_bank(c, k)[0:F, :].rearrange("f (d u j) -> f d u j", u=U, j=J))

            def x0_store(c, g):
                act.wait_ge(tr_evac, value(tr_x0T(c, GRP - 1) + 1))
                cols = slice(g * N, (g + 1) * N)
                base = (c * GRP + g) * (2 * F * N)
                act.dma_start(AP(tensor=x0_twice.tensor, offset=value(base), ap=[[N, F], [F * N, 2], [1, N]]),
                              x0T[:, cols].unsqueeze(1).broadcast_to([F, 2, N])).then_inc(x0_stored[g], 16)

            def x0R_batch(c, k):
                used = UG * 2 * (2 * (c - 1) + k + 1)
                wait(act, summed, SUMS * used)
                wait(act, scaled, ACTS * used)
                wait(act, diag_ready, J * 2 * (2 * (c - 1) + k + 1))
                evac(x0R[:, 8 * k:8 * k + 8, 0:F], tr_x0R(c, k),
                     p_top[:, 0:8 * FB].rearrange("p (u f) -> p u f", f=FB)[:, :, 0:F])

            def high(c, g, t):
                n = T1 * group(c, g) + t
                act.wait_ge(prod_ready, value(n + 1))
                wait(act, prod_used, n - 1)
                act.activation(prod_high[:, place(n, 2), :], prod[:, place(n, 2), :], ACT.Copy).then_inc(high_ready, 1)

            def x1_out(c, g):
                act.wait_ge(prod_used, value(T1 * (group(c, g) + 1)))
                wait(act, y_ready, GB * (group(c, g) - 1))
                act.activation(x1_high[:, g % 2, :], p_x1[:], ACT.Copy).then_inc(x1_high_ready, 1)

            def scale_block(c, g, u, b):
                n = unit(c, g, u)
                k = BLOCKS * u + b
                a = BY_ACT.index(b)
                act.wait_ge(y_ready, value(GB * group(c, g) + k + 1))
                if a == 0:
                    wait(act, joined, JOINS * (n - 1))
                    if g % 2 == 0 and u == 0:
                        act.wait_ge(tr_evac, value(tr_x0R(c, g // 2) + 1))
                for i in range(BF):
                    last = act.activation(scaled_y[:, u % 2, a, i, :], p_y[k % YBANKS][:, i * P:(i + 1) * P], ACT.Copy,
                                          scale=x0R[:, UG * g + u, BF * b + i:BF * b + i + 1])
                last.then_inc(scaled, 1)

            def diag(c, g, part):
                if g % 2 == 0 and part == 0:
                    act.wait_ge(tr_evac, value(tr_x0R(c, g // 2) + 1))
                for j in range(J // 4 * part, J // 4 * (part + 1)):
                    act.activation(x0_diag[:, :, j, :], x0R[:, UG * g:UG * (g + 1), :], ACT.Copy,
                                   scale=own_sample[:, j:j + 1]).then_inc(diag_ready, 1)

            def cross_out(c, g, units):
                for u in units:
                    act.wait_ge(cross_summed, value(UG * group(c, g) + u + 1))
                    at = J * (UG * g + u)
                    act.activation(cross[:, at:at + J, :].rearrange("p b f -> p (b f)"),
                                   p_cross[:, 0:J * FB], ACT.Copy).then_inc(cross_ready, 1)

            def r3_out(c):
                act.wait_ge(top_summed, value(top_use(c, 0) + 1))
                act.activation(r3[:], p_top[:, 0:P], ACT.Copy).then_inc(top_evac, 1)

            def h1_out(c):
                act.wait_ge(top_summed, value(top_use(c, 1) + 1))
                for m in range(M1):
                    last = act.activation(h1[:, m, :], p_top[:, m * P:(m + 1) * P], ACT.Relu, bias=bt1[:, m:m + 1])
                last.then_inc(top_evac, 1)

            def h2_out(c):
                act.wait_ge(top_summed, value(top_use(c, 2) + 1))
                for m in range(M2):
                    last = act.activation(h2[:, m, :], p_top[:, m * P:(m + 1) * P], ACT.Relu, bias=bt2[:, m:m + 1])
                last.then_inc(top_evac, 1)

            def y_out(c):
                act.wait_ge(top_summed, value(top_use(c, 3) + 1))
                act.activation(y_sb[:], p_top[0:1, 0:P], ACT.Copy).then_inc(top_evac, 1)
                act.wait_ge(top_evac, value(top_use(c, 3) + 1))
                act.dma_start(AP(tensor=out.tensor, offset=value(c * P), ap=[[P, 1], [1, P]]), y_sb[:]).then_inc(out_stored, 16)

            def evacuate(c, t):
                first = isinstance(c, int) and c == 0
                for k in range(GRP):
                    if t in CONTRACT_AT[k] and (k or not first):
                        cross_out(*before(c, k), (CONTRACT_AT[k].index(t),))
                if not first:
                    if t == L3_AT[-1]:
                        r3_out(c - 1)
                    if t == TOP1_AT[-1]:
                        act.wait_ge(top_in, 96)
                        h1_out(c - 1)
                    if t == TOP2_AT[-1]:
                        h2_out(c - 1)
                    if t == TOP3_AT:
                        y_out(c - 1)

            def evacuate_transposes(c, t):
                if t == X0R_SECOND_AT:
                    x0R_batch(c, 1)
                if not (isinstance(c, int) and c == LASTC):
                    if t in X0T_AT:
                        x0T_batch(c + 1, X0T_AT.index(t))
                    if t == X0R_FIRST_AT:
                        x0R_batch(c + 1, 0)

            for k in range(2):
                act.wait_ge(top_summed, k + 1)
                act.activation(dense_T[:, k * N:(k + 1) * N], p_top[0:DC, :], ACT.Copy).then_inc(top_evac, 1)
            act.wait_ge(setup_done, 6)
            act.activation(w1_high[:], f0_sb, ACT.Copy).then_inc(weights_high, 1)
            act.wait_ge(filter2_in, 16)
            act.activation(w2_high[:], f1_sb, ACT.Copy).then_inc(weights_high, 1)
            for k in range(GRP):
                x0T_batch(0, k)
            for g in range(GRP):
                x0_store(0, g)
            act.wait_ge(ones_set, 1)
            x0R_batch(0, 0)
            for t in range(T1):
                high(0, 0, t)
            x1_out(0, 0)
            act.wait_ge(weights_split, 2)

            def body(c):
                for g in range(GRP):
                    for k in range(GB):
                        t = GB * g + k
                        if k % BLOCKS in BY_ACT:
                            scale_block(c, g, k // BLOCKS, k % BLOCKS)
                        if not is_last(c, g):
                            if k in L1_HIGH:
                                high(*after(c, g), L1_HIGH.index(k))
                            if k == X1_HIGH:
                                x1_out(*after(c, g))
                        evacuate(c, t - LAG)
                        evacuate_transposes(c, t - TR_LAG)
                        if t in DIAG_AT[g]:
                            diag(c, g, DIAG_AT[g].index(t))
                        if t in STORE_AT and not (isinstance(c, int) and c == LASTC):
                            x0_store(c + 1, STORE_AT.index(t))
                if not (isinstance(c, int) and c == 0):
                    act.wait_ge(out_stored, value(16 * c))

            def end():
                cross_out(LASTC, GRP - 1, range(UG))
                r3_out(LASTC)
                h1_out(LASTC)
                h2_out(LASTC)
                y_out(LASTC)

            chunks(act, body, end)

        @block.tensor
        def _(pe):
            def x0T_waits(c, k):
                if k == 0:
                    pe.wait_ge(gathered, value(16 * F * (c + 1)))
                if not (isinstance(c, int) and c == 0):
                    if k == 0:
                        pe.wait_ge(top_evac, value(top_use(c - 1, 0)))
                    pe.wait_ge(tr_evac, value(tr_x0T(c, k)))

            def x0T_batch(c, k):
                for i in range(DB):
                    last = pe.transpose(x0T_bank(c, k)[0:F, i * P:(i + 1) * P], emb[:, :, DB * k + i], ident[:])
                last.then_inc(tr_ready, 1)

            def x0R_waits(c, k):
                pe.wait_ge(tr_evac, value(tr_x0T(c, GRP - 1) + 1))
                wait(pe, tr_evac, tr_x0R(c, k))

            def x0R_batch(c, k):
                for i in range(8):
                    u = 8 * k + i
                    last = pe.transpose(p_top[:, i * FB:i * FB + F], x0T[:, u * P:(u + 1) * P],
                                        ident[0:F, 0:F])
                last.then_inc(tr_ready, 1)

            def contract(c, g, units):
                for u in units:
                    n = unit(c, g, u)
                    if u == 0:
                        pe.wait_ge(diag_ready, value(J * (group(c, g) + 1)))
                    pe.wait_ge(joined, value(JOINS * (n + 1)))
                    wait(pe, cross_ready, n)
                    pe.matmul(p_cross[:, 0:J * FB], x2T[:, g % 2, u, :],
                              x0_diag[:, u, :, :].rearrange("p j f -> p (j f)"),
                              start=True, stop=True).then_inc(cross_summed, 1)

            def layer3(c, fields):
                for f in fields:
                    if f == 0:
                        pe.wait_ge(cross_ready, value(U * (c + 1)))
                        pe.wait_ge(filter3_in, 16)
                        pe.wait_ge(top_evac, value(top_use(c, 0)))
                        if not (isinstance(c, int) and c == LASTC):
                            pe.wait_ge(tr_evac, value(tr_x0R(c + 1, 1) + 1))
                    last = pe.matmul(p_top[:, 0:P], w3[:, f, :], cross[:, :, f], start=(f == 0), stop=(f == F - 1))
                    if f == F - 1:
                        last.then_inc(top_summed, 1)

            def top1(c, part):
                if part == 0:
                    pe.wait_ge(top_evac, value(top_use(c, 1)))
                    pe.wait_ge(r1_ready, value(c + 1))
                    pe.wait_ge(top_in, 96)
                cols = slice(part * P, (part + 1) * P)
                pe.matmul(p_top[:, cols], wt1[:, 0, cols], r1[:], start=True, stop=False)
                pe.matmul(p_top[:, cols], wt1[:, 1, cols], cross[:, :, F], start=False, stop=False)
                pe.matmul(p_top[:, cols], wt1[:, 2, cols], r3[:], start=False, stop=False)
                last = pe.matmul(p_top[:, cols], wt1_dense[:, cols], dense_T[:, bass.ds(value(c * P), P)],
                                 start=False, stop=True)
                if part == M1 - 1:
                    last.then_inc(top_summed, 1)

            def top2(c, part):
                if part == 0:
                    pe.wait_ge(top_evac, value(top_use(c, 2)))
                for k in range(M1):
                    last = pe.matmul(p_top[:, part * P:(part + 1) * P], wt2[:, k, part * P:(part + 1) * P], h1[:, k, :],
                                     start=(k == 0), stop=(k == M1 - 1))
                if part == M2 - 1:
                    last.then_inc(top_summed, 1)

            def top3(c):
                pe.wait_ge(top_evac, value(top_use(c, 3)))
                for k in range(M2):
                    last = pe.matmul(p_top[0:1, 0:P], wt3[:, k:k + 1], h2[:, k, :], start=(k == 0), stop=(k == M2 - 1))
                last.then_inc(top_summed, 1)

            def ahead(c, t):
                if t == X0R_SECOND_AT:
                    x0R_waits(c, 1)
                if isinstance(c, int) and c == LASTC:
                    return
                if t in X0T_AT:
                    x0T_waits(c + 1, X0T_AT.index(t))
                if t == X0R_FIRST_AT:
                    x0R_waits(c + 1, 0)

            def between(c, t):
                first = isinstance(c, int) and c == 0
                final = isinstance(c, int) and c == LASTC
                for k in range(GRP):
                    if t in CONTRACT_AT[k] and (k or not first):
                        contract(*before(c, k), (CONTRACT_AT[k].index(t),))
                if not first:
                    if t in L3_AT:
                        at = L3_FIELDS * L3_AT.index(t)
                        layer3(c - 1, range(at, min(at + L3_FIELDS, F)))
                    if t in TOP1_AT:
                        top1(c - 1, TOP1_AT.index(t))
                    if t in TOP2_AT:
                        top2(c - 1, TOP2_AT.index(t))
                    if t == TOP3_AT:
                        top3(c - 1)
                if t == X0R_SECOND_AT:
                    x0R_batch(c, 1)
                if not final:
                    if t in X0T_AT:
                        x0T_batch(c + 1, X0T_AT.index(t))
                    if t == X0R_FIRST_AT:
                        x0R_batch(c + 1, 0)

            def layer1(c, g, t):
                n = T1 * group(c, g) + t
                at = place(n, 2)
                if t == 0:
                    wait(pe, parts_ready, group(c, g))
                pe.wait_ge(low_ready, value(n + 1))
                pe.matmul(p_x1[:], w1_high[:, t, :], prod_high[:, at, :], start=(t == 0), stop=False)
                pe.matmul(p_x1[:], w1_low[:, t, :], prod_high[:, at, :], start=False, stop=False)
                pe.matmul(p_x1[:], w1_high[:, t, :], prod_low[:, at, :], start=False,
                          stop=(t == T1 - 1)).then_inc(prod_used, 1)

            def layer2(c, g, u, b):
                k = BLOCKS * u + b
                if k == 0:
                    pe.wait_ge(x1_low_ready, value(group(c, g) + 1))
                if not (isinstance(c, int) and GB * group(c, g) + k < YBANKS):
                    back = U * BLOCKS + BLOCKS * UG * g + k - YBANKS
                    n, old = U * (c - 1) + back // BLOCKS, back % BLOCKS
                    if old in BY_ACT:
                        pe.wait_ge(scaled, value(ACTS * n + BY_ACT.index(old) + 1))
                    else:
                        pe.wait_ge(summed, value(SUMS * n + min(BF * (BY_DVE.index(old) + 1), SUMS)))
                columns = slice(u * P, (u + 1) * P)
                fields = slice(BF * b, min(BF * (b + 1), F))
                bank = p_y[k % YBANKS][:, 0:(fields.stop - fields.start) * P]
                high, low = (w[:, fields, :].rearrange("p f m -> p (f m)") for w in (w2_high, w2_low))
                pe.matmul(bank, x1_high[:, g % 2, columns], high, start=True, stop=False)
                pe.matmul(bank, x1_high[:, g % 2, columns], low, start=False, stop=False)
                ahead(c, GB * g + k)
                pe.matmul(bank, x1_low[:, g % 2, columns], high, start=False, stop=True).then_inc(y_ready, 1)

            pe.wait_ge(ident_ready, 2)
            pe.wait_ge(dense_in, 16)
            for k in range(2):
                wait(pe, top_evac, k)
                for i in range(4):
                    last = pe.transpose(p_top[0:DC, i * P:(i + 1) * P], dense_sb[:, 4 * k + i, :], ident[:])
                last.then_inc(top_summed, 1)
            for k in range(GRP):
                x0T_waits(0, k)
                x0T_batch(0, k)
            pe.wait_ge(top_evac, 2)
            x0R_waits(0, 0)
            x0R_batch(0, 0)
            pe.wait_ge(weights_split, 2)
            for t in range(T1):
                layer1(0, 0, t)

            def body(c):
                for g in range(GRP):
                    for k in range(GB):
                        layer2(c, g, k // BLOCKS, k % BLOCKS)
                        if k in L1_MULTIPLY and not is_last(c, g):
                            layer1(*after(c, g), L1_MULTIPLY.index(k))
                        between(c, GB * g + k)

            def end():
                contract(LASTC, GRP - 1, range(UG))
                layer3(LASTC, range(F))
                for part in range(M1):
                    top1(LASTC, part)
                for part in range(M2):
                    top2(LASTC, part)
                top3(LASTC)

            chunks(pe, body, end)


def kernel(**inputs):
    import numpy as np
    import concourse.bacc as bacc
    from concourse.bass_utils import run_bass_kernel_spmd

    nc = bacc.Bacc("TRN2", target_bir_lowering=False, num_devices=1)
    arrays, handles = {}, {}
    for name, value in inputs.items():
        a = np.ascontiguousarray(value)
        arrays[f"in_{name}"] = a
        handles[name] = nc.dram_tensor(f"in_{name}", a.shape, mybir.dt.from_np(a.dtype), kind="ExternalInput").ap()
    batch, fields = inputs["ids"].shape
    out = nc.dram_tensor("out", (batch, 1), mybir.dt.float32, kind="ExternalOutput").ap()
    build_cin_tower(nc, handles["dense_ctx"], handles["ids"], [handles[f"tbl_{f}"] for f in range(fields)],
                    handles["W_top1"], handles["b_top1"], handles["W_top2"], handles["b_top2"], handles["W_top3"],
                    handles["L0_rec_f0"], handles["L0_rec_f1"], handles["L0_rec_f2"], out)
    r = run_bass_kernel_spmd(nc, [arrays], core_ids=[0])
    return r.results[0]["out"]
```
